# Optimizing a Trainium2 kernel written in Bass

```python
import numpy as np
import jax
import jax.numpy as jnp

def _softmax(x, axis=-1):
    return jax.nn.softmax(x, axis=axis)

def _gelu(x):
    return jax.nn.gelu(x, approximate=True)

def _silu(x):
    return jax.nn.silu(x)

def _sigmoid(x):
    return jax.nn.sigmoid(x)

def _layernorm(x, axis=-1, eps=1e-05):
    m = jnp.mean(x, axis=axis, keepdims=True)
    v = jnp.var(x, axis=axis, keepdims=True)
    return (x - m) / jnp.sqrt(v + eps)

def _scatter_add(tgt, idx, src, axis=0):
    return tgt.at[idx].add(src)

def _segment_sum(src, seg, n):
    return jax.ops.segment_sum(src, seg, n)
kernel_name = 'mk_decoder_preln_d1_seqx_r8_63360c'

def setup_inputs(seed: int=0):
    np.random.seed(seed)
    _w = jnp.asarray

    def _rec_inputs():
        import jax
        import jax.numpy as jnp
        _rk = jax.random.key(seed)
        x = -0.0002928 + 1 * jax.random.normal(jax.random.fold_in(_rk, 1), (4, 256, 128), jnp.float32)
        _lenS = 256 - jax.random.randint(jax.random.fold_in(_rk, 7), (4,), 0, max(1, 256 // 4) + 1, jnp.int32)
        _lenS2 = 512 - jax.random.randint(jax.random.fold_in(_rk, 8), (4,), 0, max(1, 512 // 4) + 1, jnp.int32)
        _ctx_1024P = jax.random.normal(jax.random.fold_in(_rk, 11), (4, 16, 128), jnp.float32)
        _ctx_1024c = jax.random.dirichlet(jax.random.fold_in(_rk, 511), 0.3 * jnp.ones((16,), jnp.float32), (4, 512))
        _ctx_1024t = jnp.einsum('bsk,bkd->bsd', _ctx_1024c, _ctx_1024P)
        _ctx_1024t = _ctx_1024t * jax.lax.rsqrt(jnp.mean(jnp.square(_ctx_1024t)) + 1e-12) * 0.953939
        ctx_1024 = 2.81802e-05 + 1.00001 * (_ctx_1024t + 0.3 * jax.random.normal(jax.random.fold_in(_rk, 611), (4, 512, 128), jnp.float32))
        _validS = jnp.arange(256)[None, :] < _lenS[:, None]
        _validS2 = jnp.arange(512)[None, :] < _lenS2[:, None]
        _causal = jnp.tril(jnp.ones((256, 256), dtype=bool))
        mask_BxS2_bk0 = jnp.logical_not(jnp.broadcast_to(_validS2[:, :], (4, 512)))
        return (x, ctx_1024, mask_BxS2_bk0)
    x, ctx_1024, mask_BxS2_bk0 = _rec_inputs()

    def _L0_attn_setup():
        import jax, jax.numpy as jnp
        import numpy as np
        B, N, C = (4, 256, 128)
        H = 16
        D = C // H
        SCALE = D ** (-0.5)
        key = jax.random.key(seed)
        ks = jax.random.split(key, 5)
        x = jax.random.normal(ks[0], (B, N, C), dtype=jnp.float32)
        w_qkv = jax.random.normal(ks[1], (3 * C, C), dtype=jnp.float32) * C ** (-0.5)
        b_qkv = jax.random.normal(ks[2], (3 * C,), dtype=jnp.float32) * 0.02
        w_proj = jax.random.normal(ks[3], (C, C), dtype=jnp.float32) * C ** (-0.5)
        b_proj = jax.random.normal(ks[4], (C,), dtype=jnp.float32) * 0.02
        return {'x': x, 'w_qkv': w_qkv, 'b_qkv': b_qkv, 'w_proj': w_proj, 'b_proj': b_proj}
    _L0_attn_all = _L0_attn_setup()
    _L0_attn_in = {k: v for k, v in _L0_attn_all.items() if k in ('w_qkv', 'b_qkv', 'w_proj', 'b_proj')}
    del _L0_attn_all

    def _L0_xattn_setup():
        import jax, jax.numpy as jnp
        import numpy as np
        NUM_HEADS, NUM_KV, HEAD_DIM, WIDTH = (4, 1, 32, 128)
        MASK_FILL = -2.3819763e+38

        def _apply_rope(x, positions, max_wavelength=10000.0):
            d = x.shape[-1]
            freq_exp = 2.0 / d * jnp.arange(d // 2, dtype=jnp.float32)
            timescale = max_wavelength ** freq_exp
            radians = positions[..., None].astype(jnp.float32) / timescale
            radians = radians[..., None, :]
            sin, cos = (jnp.sin(radians), jnp.cos(radians))
            x1, x2 = jnp.split(x, 2, axis=-1)
            out = jnp.concatenate([x1 * cos - x2 * sin, x2 * cos + x1 * sin], axis=-1)
            return out.astype(x.dtype)

        def _rmsnorm(x, scale):
            var = jnp.mean(jnp.square(x.astype(jnp.float32)), axis=-1, keepdims=True)
            normed = x * jax.lax.rsqrt(var + 1e-06)
            return (normed * (1 + scale)).astype(x.dtype)
        key = jax.random.key(seed)
        ks = jax.random.split(key, 7)
        B, T, S = (8, 64, 256)
        return {'x': jax.random.normal(ks[0], (B, T, WIDTH), jnp.float32), 'mem_seq': jax.random.normal(ks[1], (B, S, WIDTH), jnp.float32), 'mem_mask': jax.random.randint(ks[2], (B, S), 0, 2).astype(bool), 'rms_scale': jax.random.normal(ks[3], (WIDTH,), jnp.float32) * 0.02, 'q_w': jax.random.normal(ks[4], (NUM_HEADS, WIDTH, HEAD_DIM), jnp.float32) / np.sqrt(WIDTH), 'kv_w': jax.random.normal(ks[5], (2, NUM_KV, WIDTH, HEAD_DIM), jnp.float32) / np.sqrt(WIDTH), 'out_w': jax.random.normal(ks[6], (NUM_HEADS, HEAD_DIM, WIDTH), jnp.float32) / np.sqrt(NUM_HEADS * HEAD_DIM)}
    _L0_xattn_all = _L0_xattn_setup()
    _L0_xattn_in = {k: v for k, v in _L0_xattn_all.items() if k in ('rms_scale', 'q_w', 'kv_w', 'out_w')}
    del _L0_xattn_all

    def _L0_ffn_setup():
        import jax, jax.numpy as jnp
        import numpy as np
        B, S, H, F, E = (4, 256, 128, 512, 8)
        key = jax.random.key(seed)
        ks = jax.random.split(key, 8)
        s = 1.0 / np.sqrt(H)
        sf = 1.0 / np.sqrt(F)
        return {'x': jax.random.normal(ks[0], (B, S, H), jnp.float32), 'wr': jax.random.uniform(ks[1], (H, E), jnp.float32, -s, s), 'br': jax.random.uniform(ks[2], (E,), jnp.float32, -s, s), 'w1': jax.random.uniform(ks[3], (E, H, F), jnp.float32, -s, s), 'b1': jax.random.uniform(ks[4], (E, F), jnp.float32, -s, s), 'w2': jax.random.uniform(ks[5], (E, F, H), jnp.float32, -sf, sf), 'b2': jax.random.uniform(ks[6], (E, H), jnp.float32, -sf, sf)}
    _L0_ffn_all = _L0_ffn_setup()
    _L0_ffn_in = {k: v for k, v in _L0_ffn_all.items() if k in ('wr', 'br', 'w1', 'b1', 'w2', 'b2')}
    del _L0_ffn_all
    return {'x': x, 'ctx_1024': ctx_1024, 'mask_BxS2_bk0': mask_BxS2_bk0, 'L0_attn_w_qkv': _L0_attn_in['w_qkv'], 'L0_attn_b_qkv': _L0_attn_in['b_qkv'], 'L0_attn_w_proj': _L0_attn_in['w_proj'], 'L0_attn_b_proj': _L0_attn_in['b_proj'], 'L0_xattn_rms_scale': _L0_xattn_in['rms_scale'], 'L0_xattn_q_w': _L0_xattn_in['q_w'], 'L0_xattn_kv_w': _L0_xattn_in['kv_w'], 'L0_xattn_out_w': _L0_xattn_in['out_w'], 'L0_ffn_wr': _L0_ffn_in['wr'], 'L0_ffn_br': _L0_ffn_in['br'], 'L0_ffn_w1': _L0_ffn_in['w1'], 'L0_ffn_b1': _L0_ffn_in['b1'], 'L0_ffn_w2': _L0_ffn_in['w2'], 'L0_ffn_b2': _L0_ffn_in['b2']}

def reference(x, ctx_1024, mask_BxS2_bk0, L0_attn_w_qkv, L0_attn_b_qkv, L0_attn_w_proj, L0_attn_b_proj, L0_xattn_rms_scale, L0_xattn_q_w, L0_xattn_kv_w, L0_xattn_out_w, L0_ffn_wr, L0_ffn_br, L0_ffn_w1, L0_ffn_b1, L0_ffn_w2, L0_ffn_b2):
    import jax
    import jax.numpy as jnp

    def _L0_attn_ref(x, w_qkv, b_qkv, w_proj, b_proj):
        import jax, jax.numpy as jnp
        import numpy as np
        B, N, C = (4, 256, 128)
        H = 16
        D = C // H
        SCALE = D ** (-0.5)
        b, n, c = x.shape
        qkv = (x @ w_qkv.T + b_qkv).reshape(b, n, 3, H, D).transpose(2, 0, 3, 1, 4)
        q, k, v = (qkv[0], qkv[1], qkv[2])
        attn = jnp.einsum('bhnd,bhmd->bhnm', q, k) * SCALE
        attn = jax.nn.softmax(attn, axis=-1)
        out = jnp.einsum('bhnm,bhmd->bhnd', attn, v)
        out = out.transpose(0, 2, 1, 3).reshape(b, n, c)
        return out @ w_proj.T + b_proj

    def _L0_xattn_ref(x, mem_seq, mem_mask, rms_scale, q_w, kv_w, out_w):
        import jax, jax.numpy as jnp
        import numpy as np
        NUM_HEADS, NUM_KV, HEAD_DIM, WIDTH = (4, 1, 32, 128)
        MASK_FILL = -2.3819763e+38

        def _apply_rope(x, positions, max_wavelength=10000.0):
            d = x.shape[-1]
            freq_exp = 2.0 / d * jnp.arange(d // 2, dtype=jnp.float32)
            timescale = max_wavelength ** freq_exp
            radians = positions[..., None].astype(jnp.float32) / timescale
            radians = radians[..., None, :]
            sin, cos = (jnp.sin(radians), jnp.cos(radians))
            x1, x2 = jnp.split(x, 2, axis=-1)
            out = jnp.concatenate([x1 * cos - x2 * sin, x2 * cos + x1 * sin], axis=-1)
            return out.astype(x.dtype)

        def _rmsnorm(x, scale):
            var = jnp.mean(jnp.square(x.astype(jnp.float32)), axis=-1, keepdims=True)
            normed = x * jax.lax.rsqrt(var + 1e-06)
            return (normed * (1 + scale)).astype(x.dtype)
        B, S, _ = mem_seq.shape
        T = x.shape[1]
        G = NUM_HEADS // NUM_KV
        xn = _rmsnorm(x, rms_scale)
        mn = _rmsnorm(mem_seq, rms_scale)
        q = jnp.einsum('BTD,NDH->BTNH', xn, q_w)
        kv = jnp.einsum('BSD,cKDH->cBSKH', mn, kv_w)
        k, v = (kv[0], kv[1])
        q_pos = jnp.broadcast_to(jnp.arange(S, T + S), (B, T))
        k_pos = jnp.broadcast_to(jnp.arange(S), (B, S))
        q = _apply_rope(q, q_pos) * HEAD_DIM ** (-0.5)
        k = _apply_rope(k, k_pos)
        q = q.reshape(B, T, NUM_KV, G, HEAD_DIM)
        logits = jnp.einsum('BTKGH,BSKH->BKGTS', q, k, preferred_element_type=jnp.float32)
        masked = jnp.where(mem_mask[:, None, None, None, :], logits, MASK_FILL)
        probs = jax.nn.softmax(masked, axis=-1).astype(x.dtype)
        enc = jnp.einsum('BKGTS,BSKH->BTKGH', probs, v).reshape(B, T, NUM_HEADS, HEAD_DIM)
        return jnp.einsum('BTNH,NHD->BTD', enc, out_w)

    def _L0_ffn_ref(x, wr, br, w1, b1, w2, b2):
        import jax, jax.numpy as jnp
        import numpy as np
        B, S, H, F, E = (4, 256, 128, 512, 8)
        scores = jnp.einsum('bsh,he->bse', x, wr) + br
        expert_id = jnp.argmax(scores, axis=-1)
        h = jnp.einsum('bsh,ehf->ebsf', x, w1) + b1[:, None, None, :]
        h = jax.nn.gelu(h, approximate=False)
        y = jnp.einsum('ebsf,efh->ebsh', h, w2) + b2[:, None, None, :]
        one_hot = jax.nn.one_hot(expert_id, E, dtype=x.dtype)
        out = jnp.einsum('ebsh,bse->bsh', y, one_hot)
        return out
    x = x + _L0_attn_ref(_layernorm(x, axis=-1), L0_attn_w_qkv, L0_attn_b_qkv, L0_attn_w_proj, L0_attn_b_proj)
    x = x + _L0_xattn_ref(_layernorm(x, axis=-1), ctx_1024, mask_BxS2_bk0, L0_xattn_rms_scale, L0_xattn_q_w, L0_xattn_kv_w, L0_xattn_out_w)
    x = x + _L0_ffn_ref(_layernorm(x, axis=-1), L0_ffn_wr, L0_ffn_br, L0_ffn_w1, L0_ffn_b1, L0_ffn_w2, L0_ffn_b2)
    return x

_drawn_inputs = setup_inputs


def setup_inputs(seed=0):
    import zlib

    import numpy as np

    out = dict(_drawn_inputs(seed))
    spreads = {}
    factors = {'L0_xattn_rms_scale': 2.682, 'L0_ffn_b1': 3.704}
    for name, (base, spread) in spreads.items():
        noise = np.random.default_rng([zlib.crc32(name.encode()), seed]).standard_normal(out[name].shape)
        drawn = base * np.exp(spread * noise) if base else spread * noise
        out[name] = jnp.asarray(drawn.astype(out[name].dtype))
    for name, factor in factors.items():
        out[name] = (out[name] * factor).astype(out[name].dtype)
    return out
```

```python
from contextlib import ExitStack

import concourse.bass as bass
import concourse.mybir as mybir
import numpy as np

F32 = mybir.dt.float32
BF16 = mybir.dt.bfloat16
I32 = mybir.dt.int32
U8 = mybir.dt.uint8
ALU = mybir.AluOpType
ACT = mybir.ActivationFunctionType
AX = mybir.AxisListType

B, N, C = 4, 256, 128
H, D = 16, 8
M = 512
XH, XD = 4, 32
E, F = 8, 512
P = 128
NT = N // P
TT = B * NT
MT = M // P
PAIRS = H // 2
CHUNKS = NT * PAIRS
XCHUNKS = NT * XH
LEAD = 6
XAHEAD = {(1, 0): range(16, 20), (1, 1): range(20, 24), (2, 0): range(24, 28), (2, 1): range(28, 32)}
SCALE = D ** -0.5
LN_EPS = 1e-5
RMS_EPS = 1e-6
MASK_FILL = -2.3819763e38
FT = F // P
BLOCKS = TT + E - 1
SLOTS = BLOCKS * P

ROW = (0, 8, 16, 24, 40, 48)
MAX_ROW = 32
Q_COPIES = ((ROW[0], 3, 0), (ROW[3], 1, 0), (ROW[4], 2, 0))
K_COPIES = ((ROW[0], 3, 0), (ROW[3], 1, 2), (ROW[4], 2, 1))
XQ_COPIES = ((0, 0, 3, 0), (1, 0, 2, 0), (1, 2 * XD, 1, 0))
XK_COPIES = ((0, 0, 3, 0), (1, 0, 2, 1), (1, 2 * XD, 1, 2))
XMAX_ROW = 96
ONE_ONE = 0x3F803F80


def build(nc, a):
    ctx = ExitStack()
    with ctx:
        def sb(name, shape, dt=F32):
            return ctx.enter_context(nc.sbuf_tensor(name, shape, dt))

        def sem(name):
            return ctx.enter_context(nc.semaphore(name))

        qk_scratch = nc.dram_tensor("qk_scratch", [B, 3, 2, P, N], BF16).ap()
        max_scratch = nc.dram_tensor("max_scratch", [B, 3, 2, PAIRS, N], BF16).ap()
        xmax_scratch = nc.dram_tensor("xmax_scratch", [B, 3, XH, N], BF16).ap()
        mask_scratch = nc.dram_tensor("mask_scratch", [B, M], BF16).ap()
        xq_scratch = nc.dram_tensor("xq_scratch", [B, 3, P, N], BF16).ap()
        xk_scratch = nc.dram_tensor("xk_scratch", [P, 3, M], BF16).ap()
        sorted_in = nc.dram_tensor("sorted_in", [SLOTS, C], F32).ap()
        sorted_out = nc.dram_tensor("sorted_out", [SLOTS, C], F32).ap()

        x = sb("x", [P, TT, C])
        xn = sb("xn", [P, TT, C])
        xnT = sb("xnT", [P, TT, P])
        stats = sb("stats", [P, TT, 6])
        mv = sb("mv", [P, TT, 2])
        var_eps = sb("var_eps", [P, TT])
        rstd = sb("rstd", [P, TT])
        w2nd = sb("w2nd", [P, TT])
        half = sb("half", [P, 16])
        ident = sb("ident", [P, P])
        ident_b = sb("ident_b", [P, P], BF16)
        wqk = sb("wqk", [P, 2, P])
        wv = sb("wv", [P, P])
        bqk = sb("bqk", [P, 2])
        bqk_s = sb("bqk_s", [P, 2])
        bv = sb("bv", [P, NT, P])
        wproj = sb("wproj", [P, 2, P])
        spread = sb("spread", [P, P])
        qk_f = sb("qk_f", [P, 2, 2, N])
        qk_r = sb("qk_r", [P, 2 * N])
        qk_parts = sb("qk_parts", [P, B, 3, 2, N], BF16)
        q_st = sb("q_st", [P, B, PAIRS, N], BF16)
        k_bd = sb("k_bd", [P, B, 2, PAIRS, N], BF16)
        v_aug = sb("v_aug", [P, B, NT * PAIRS, 2, 32])
        probs = sb("probs", [P, 8, 1024])
        neg_max = sb("neg_max", [P, 2, NT, 2, PAIRS])
        max_r = sb("max_r", [P, NT * H])
        max_parts = sb("max_parts", [P, 2, NT, 3, H], BF16)
        max_t = sb("max_t", [3 * H, 2, N], BF16)
        o_sb = sb("o_sb", [P, 2, N])
        rec = sb("rec", [P, 2, N])
        o_n = sb("o_n", [P, 2, N])
        mem = sb("mem", [P, B * MT, C])
        memT = probs[:, 6:8, :].rearrange("p s (t n) -> p (s t) n", n=P)
        mem_ss = sb("mem_ss", [P, B * MT])
        mem_rs = sb("mem_rs", [P, B * MT])
        squares = probs[:, 4:6, :].rearrange("p s (t n) -> p (s t) n", n=P)
        rms_scale = sb("rms_scale", [P, 1])
        xw = sb("xw", [P, 2 * P + 3 * XD])
        xws = sb("xws", [P, 2 * P + 3 * XD])
        wout = sb("wout", [P, C])
        rope_q = sb("rope_q", [P, 2, N])
        rope_k = sb("rope_k", [P, 2, M])
        mask_u8 = sb("mask_u8", [P, M], U8)
        mask_f = sb("mask_f", [P, M])
        mask_row = sb("mask_row", [P, M], BF16)
        any_on = sb("any_on", [P, 1])
        xk_t = sb("xk_t", [P, 2, M])
        xk_parts = sb("xk_parts", [P, 3, M], BF16)
        xv_t = sb("xv_t", [P, M])
        xv = sb("xv", [P, MT, B, XD])
        ones = sb("ones", [P, XD])
        kx = [sb(f"kx{i}", [P, B, M], BF16) for i in range(2)]
        qx = [sb(f"qx{i}", [P, B, XH, N], BF16) for i in range(2)]
        xq_t = sb("xq_t", [P, 2, N])
        xq_parts = sb("xq_parts", [P, 2, 3, N], BF16)
        xneg_max = sb("xneg_max", [P, 2, NT, XH])
        xmax_r = sb("xmax_r", [P, NT * XH])
        xmax_parts = sb("xmax_parts", [P, 2, NT, 3, XH], BF16)
        xmax_t = sb("xmax_t", [3 * XH, 2, N], BF16)

        w1 = k_bd[:].rearrange("p b i r n -> p (b i r n)").bitcast(F32)[:, 0:E * F]
        w2 = k_bd[:].rearrange("p b i r n -> p (b i r n)").bitcast(F32)[:, E * F:2 * E * F]
        b1 = q_st[:].rearrange("p b r n -> p (b r n)").bitcast(F32)
        v_flat = v_aug[:].rearrange("p b t i n -> p (b t i n)")
        b2 = v_flat[:, 0:E * C]
        xs = v_flat[:, E * C:E * C + BLOCKS * C].rearrange("p (j c) -> p j c", c=C)
        xsT = sb("xsT", [P, 2, P])
        hid = probs[:, 0]
        act_h = probs[:, 1]
        act_T = probs[:, 2]
        ys = probs[:, 3, 0:2 * C]
        yg = probs[:, 4:6, :].rearrange("p s (t n) -> p (s t) n", n=C)
        wr = sb("wr", [P, E])
        br = sb("br", [P, E])
        route_c = sb("route_c", [P, 3 * 64 + BLOCKS * E])
        tri = sb("tri", [P, P], BF16)
        ones_b = sb("ones_b", [P, P], BF16)
        sc = sb("sc", [P, TT, E])
        cand = sb("cand", [P, TT, E])
        top = sb("top", [P, 2, TT])
        one_hot = sb("one_hot", [P, TT, E], BF16)
        blk = sb("blk", [P, 3, E])
        blk_t = sb("blk_t", [P, BLOCKS, E])
        blk_f = sb("blk_f", [P, BLOCKS])
        block_expert = sb("block_expert", [P, BLOCKS], I32)
        slot_f = sb("slot_f", [P, TT])
        slot = sb("slot", [P, TT], I32)

        ps = ctx.enter_context(nc.psum_tensor("ps", [P, 8, 512], F32))
        s_ring = [ps[:, i, :] for i in range(2)]
        t_ring = [ps[:, 2 + i, :] for i in range(3)]
        o_ps = [ps[:, 5 + i, :] for i in range(2)]
        misc = ps[:, 7, :]

        x_in = [sem(f"x_in{b}") for b in range(B)]
        c_in = sem("c_in")
        c2_in = sem("c2_in")
        c3_in = sem("c3_in")
        mem_in = sem("mem_in")
        dve_step = sem("dve_step")
        act_step = sem("act_step")
        pool_step = sem("pool_step")
        pool_const = sem("pool_const")
        k_zero = sem("k_zero")
        zeroed = sem("zeroed")
        var_ok = sem("var_ok")
        rstd_ok = sem("rstd_ok")
        xn_ok = sem("xn_ok")
        xT_ps = sem("xT_ps")
        xT_ok = sem("xT_ok")
        qk_ps = sem("qk_ps")
        v_ps = sem("v_ps")
        qk_fok = sem("qk_fok")
        v_ok = sem("v_ok")
        parts_ok = sem("parts_ok")
        parts_out = [sem(f"parts_out{b}") for b in range(B)]
        stacked = [sem(f"stacked{b}") for b in range(B)]
        s_ready = sem("s_ready")
        max_ok = sem("max_ok")
        mparts_ok = sem("mparts_ok")
        mT_ps = sem("mT_ps")
        mT_ok = sem("mT_ok")
        max_out = [sem(f"max_out{b}") for b in range(2 * B)]
        max_in = [sem(f"max_in{b}") for b in range(2 * B)]
        t_ready = sem("t_ready")
        exp_ok = sem("exp_ok")
        pv_ok = sem("pv_ok")
        o_ok = sem("o_ok")
        den_ps = sem("den_ps")
        rec_ok = sem("rec_ok")
        on_ok = sem("on_ok")
        proj_ps = sem("proj_ps")
        x_ok = sem("x_ok")
        sq_ok = sem("sq_ok")
        mem_rs_ok = sem("mem_rs_ok")
        mem_n_ok = sem("mem_n_ok")
        memT_ps = sem("memT_ps")
        memT_ok = sem("memT_ok")
        kv_ps = sem("kv_ps")
        xk_ok = sem("xk_ok")
        xvt_ok = sem("xvt_ok")
        xv_ps = sem("xv_ps")
        xv_ok = sem("xv_ok")
        xk_out = sem("xk_out")
        xk_in = sem("xk_in")
        xws_ok = sem("xws_ok")
        xq_ps = sem("xq_ps")
        xrope_ok = sem("xrope_ok")
        xq_ok = sem("xq_ok")
        xq_out = [sem(f"xq_out{b}") for b in range(B)]
        xq_in = [sem(f"xq_in{b}") for b in range(B)]
        xpv_ok = sem("xpv_ok")
        xon_ok = sem("xon_ok")
        ffn_in = sem("ffn_in")
        route_in = sem("route_in")
        xT3_ps = sem("xT3_ps")
        score_ps = sem("score_ps")
        hot_ok = sem("hot_ok")
        rank_ps = sem("rank_ps")
        slot_ok = sem("slot_ok")
        table_ok = sem("table_ok")
        filled = sem("filled")
        scattered = [sem(f"scattered{t}") for t in range(TT)]
        xs_in = [sem(f"xs_in{i}") for i in range(3)]
        xsT_ps = sem("xsT_ps")
        xsT_ok = sem("xsT_ok")
        h_ps = sem("h_ps")
        h_ok = sem("h_ok")
        g_ok = sem("g_ok")
        gT_ps = sem("gT_ps")
        gT_ok = sem("gT_ok")
        y_ps = sem("y_ps")
        y_ok = sem("y_ok")
        y_out = [sem(f"y_out{i}") for i in range(2)]
        gathered = [sem(f"gathered{t}") for t in range(TT)]
        out_done = sem("out_done")
        act_ident = sem("act_ident")

        block = ctx.enter_context(nc.Block())
        W1 = 6 * 16
        W2 = 4 * 16
        W3 = 3 * 16

        @block.sync
        def _(sp):
            sp.dma_start(x[:, 0:NT, :], a["x"][0]).then_inc(x_in[0], 16)
            sp.dma_start(ident[:], a["ident"]).then_inc(c_in, 16)
            sp.dma_start(wqk[:], a["wqk"]).then_inc(c_in, 16)
            sp.dma_start(bqk[:], a["bqk"]).then_inc(c_in, 16)
            for b in range(1, B):
                sp.dma_start(x[:, NT * b:NT * b + NT, :], a["x"][b]).then_inc(x_in[b], 16)
            sp.dma_start(wv[:], a["wv"]).then_inc(c_in, 16)
            sp.dma_start(bv[:], a["bv"]).then_inc(c_in, 16)
            sp.dma_start(spread[:], a["spread"]).then_inc(c_in, 16)
            sp.dma_start(mem[:], a["mem"]).then_inc(mem_in, 16)
            for dst, name in ((rms_scale, "rms_scale"), (xw, "xw"), (rope_k, "rope_k"), (mask_u8, "mask")):
                sp.dma_start(dst[:], a[name]).then_inc(c2_in, 16)

            def write_parts(b):
                sp.wait_ge(parts_ok, b + 1)
                sp.dma_start(qk_scratch[b].rearrange("s t p n -> p s t n"), qk_parts[:, b]).then_inc(parts_out[b], 16)

            def stack(b):
                sp.wait_ge(parts_out[b], 16)
                sp.wait_ge(zeroed, b + 1)
                for i in range(2):
                    rows = qk_scratch[b].rearrange("s t (d j r) n -> s t j d (r n)", j=2, r=PAIRS)
                    for row, copies, part in Q_COPIES:
                        r = 64 * i + row
                        dst = q_st[r:r + D * copies, b].rearrange("p r n -> p (r n)")
                        sp.dma_start(dst, rows[part:part + copies, 0, i]).then_inc(stacked[b], 16)
                    for row, copies, part in K_COPIES:
                        r = 64 * i + row
                        dst = k_bd[r:r + D * copies, b, i].rearrange("p r n -> p (r n)")
                        src = rows[part:part + 1, 1, i].to_broadcast([copies, D, PAIRS * N])
                        sp.dma_start(dst, src).then_inc(stacked[b], 16)

            write_parts(0)
            stack(0)
            write_parts(1)
            stack(1)
            write_parts(2)
            write_parts(3)
            stack(2)
            for dst, name in ((rope_q, "rope_q"), (wout, "wout"), (wproj, "wproj")):
                sp.dma_start(dst[:], a[name]).then_inc(c3_in, 16)

            def max_rows(b):
                sp.wait_ge(mT_ok, b + 1)
                sp.dma_start(max_scratch[b].rearrange("s i r n -> (s i r) n"), max_t[:, b % 2]).then_inc(max_out[b], 16)
                sp.wait_ge(max_out[b], 16)
                for i in range(2):
                    r = 64 * i + MAX_ROW
                    sp.dma_start(q_st[r:r + 3, b], max_scratch[b, :, i]).then_inc(max_in[b], 16)

            def cross_k():
                sp.wait_ge(xk_ok, 1)
                sp.dma_start(xk_scratch, xk_parts[:]).then_inc(xk_out, 16)
                sp.dma_start(mask_scratch, mask_row[0:P:XD]).then_inc(xk_out, 16)
                sp.wait_ge(xk_out, 32)
                src = xk_scratch.rearrange("(b d) s m -> s d b m", d=XD)
                for j, row, copies, part in XK_COPIES:
                    for s in range(copies):
                        r = row + XD * s
                        sp.dma_start(kx[j][r:r + XD], src[part]).then_inc(xk_in, 16)
                sp.dma_start(kx[1][XMAX_ROW:XMAX_ROW + 1], mask_scratch.unsqueeze(0)).then_inc(xk_in, 16)

            def cross_q(b):
                sp.wait_ge(xq_ok, b + 1)
                sp.dma_start(xq_scratch[b].rearrange("s p n -> p s n"), xq_parts[:, b % 2]).then_inc(xq_out[b], 16)
                sp.wait_ge(xq_out[b], 16)
                src = xq_scratch[b].rearrange("s (d h) n -> (s d) (h n)", h=XH)
                for j, row, copies, part in XQ_COPIES:
                    sp.dma_start(qx[j][row:row + XD * copies, b].rearrange("p h n -> p (h n)"),
                                 src[XD * part:XD * (part + copies)]).then_inc(xq_in[b], 16)

            def xmax_rows(b):
                sp.wait_ge(mT_ok, B + b + 1)
                sp.dma_start(xmax_scratch[b].rearrange("s h n -> (s h) n"), xmax_t[:, b % 2]).then_inc(max_out[B + b], 16)
                sp.wait_ge(max_out[B + b], 16)
                sp.dma_start(qx[0][XMAX_ROW:XMAX_ROW + 3, b], xmax_scratch[b]).then_inc(max_in[B + b], 16)

            max_rows(0)
            stack(3)
            cross_k()
            sp.dma_start(sorted_in, a["zeros"]).then_inc(filled, 16)
            for dst, name in ((wr, "wr"), (br, "br"), (route_c, "route_c"), (tri, "tri"), (ones_b, "ones_b")):
                sp.dma_start(dst[:], a[name]).then_inc(route_in, 16)
            max_rows(1)
            max_rows(2)
            cross_q(0)
            max_rows(3)
            cross_q(1)
            xmax_rows(0)
            cross_q(2)
            xmax_rows(1)
            sp.wait_ge(exp_ok, B * H)
            sp.wait_ge(pv_ok, 2 * B)
            sp.dma_start(w1, a["w1"]).then_inc(ffn_in, 16)
            cross_q(3)
            xmax_rows(2)
            sp.dma_start(w2, a["w2"]).then_inc(ffn_in, 16)
            xmax_rows(3)
            sp.dma_start(b1, a["b1"]).then_inc(ffn_in, 16)
            sp.dma_start(b2, a["b2"]).then_inc(ffn_in, 16)
            for t in range(TT):
                sp.wait_ge(scattered[t], 16)
            for i in range(3):
                j = i * BLOCKS // 3
                n = BLOCKS // 3
                sp.dma_start(xs[:, j:j + n], sorted_in[P * j:P * (j + n)].rearrange("(j p) c -> p j c", p=P))\
                    .then_inc(xs_in[i], 16)
            for j in range(BLOCKS):
                sp.wait_ge(y_ok, j + 1)
                sp.dma_start(sorted_out[P * j:P * j + P], ys[:, C * (j % 2):C * (j % 2) + C]).then_inc(y_out[j % 2], 16)
            for b in range(B):
                sp.wait_ge(x_ok, 2 * B + b + 1)
                sp.dma_start(a["out"][b], x[:, NT * b:NT * b + NT, :]).then_inc(out_done, 16)
            sp.wait_ge(out_done, 16 * B)

        @block.gpsimd
        def _(pool):
            steps = [0]

            def chain(ins):
                steps[0] += 1
                ins.then_inc(pool_step, 1)
                pool.wait_ge(pool_step, steps[0])

            pool.memset(half[:], -0.5).then_inc(pool_const, 1)
            pool.wait_ge(pool_const, 1)

            def power(b, first):
                t = slice(NT * b, NT * b + NT)
                pool.wait_ge(var_ok, first + b + 1)
                if first == B:
                    chain(pool.tensor_tensor(rstd[:, t], var_eps[:, t], half[:, 0:NT], ALU.pow))
                    chain(pool.tensor_tensor(w2nd[:, t], rstd[:, t], rstd[:, t], ALU.mult))
                    chain(pool.tensor_tensor(w2nd[:, t], w2nd[:, t], mv[:, t, 1], ALU.mult))
                    chain(pool.tensor_scalar(w2nd[:, t], w2nd[:, t], RMS_EPS, None, ALU.add))
                    chain(pool.tensor_tensor(w2nd[:, t], w2nd[:, t], half[:, 0:NT], ALU.pow))
                    pool.tensor_tensor(rstd[:, t], rstd[:, t], w2nd[:, t], ALU.mult).then_inc(rstd_ok, 1)
                else:
                    pool.tensor_tensor(rstd[:, t], var_eps[:, t], half[:, 0:NT], ALU.pow).then_inc(rstd_ok, 1)
                pool.wait_ge(rstd_ok, first + b + 1)

            def zero(b):
                if b:
                    chain(pool.memset(q_st[:, b].bitcast(F32), 0.0))
                pool.wait_ge(k_zero, b + 1)
                chain(pool.memset(k_bd[MAX_ROW:MAX_ROW + 3, b, 0].bitcast(I32), ONE_ONE))
                pool.memset(k_bd[64 + MAX_ROW:64 + MAX_ROW + 3, b, 1].bitcast(I32), ONE_ONE).then_inc(zeroed, 1)
                pool.wait_ge(zeroed, b + 1)

            def zero_v(half):
                b = slice(2 * half, 2 * half + 2)
                chain(pool.memset(v_aug[:, b], 0.0))
                chain(pool.memset(v_aug[:, b, :, 0, 16:17], 1.0))
                pool.memset(v_aug[:, b, :, 1, 17:18], 1.0).then_inc(pool_const, 1)
                pool.wait_ge(pool_const, 2 + half)

            def normalise(b, g):
                pool.wait_ge(o_ok, 2 * b + g + 1)
                pool.wait_ge(rec_ok, 2 * b + g + 1)
                if b >= 1:
                    pool.wait_ge(proj_ps, b)
                pool.tensor_tensor(o_n[:, g], o_sb[:, g], rec[:, g], ALU.mult).then_inc(on_ok, 1)
                pool.wait_ge(on_ok, 2 * b + g + 1)

            power(0, 0)
            power(1, 0)
            zero(0)
            power(2, 0)
            power(3, 0)
            zero(1)
            zero(2)
            zero(3)
            zero_v(0)
            zero_v(1)
            chain(pool.memset(ones[:], 1.0))
            chain(pool.memset(kx[0][XMAX_ROW:XMAX_ROW + 3], 1.0))
            pool.memset(qx[1][XMAX_ROW:XMAX_ROW + 1], 1.0).then_inc(pool_const, 1)
            pool.wait_ge(pool_const, 4)
            pool.wait_ge(sq_ok, 1)
            chain(pool.tensor_scalar(mem_rs[:], mem_ss[:], 1.0 / C, RMS_EPS, ALU.mult, ALU.add))
            chain(pool.tensor_tensor(mem_rs[:], mem_rs[:], half[:, 0:B * MT], ALU.pow))
            pool.tensor_tensor(mem[:], mem[:], mem_rs[:].unsqueeze(2).to_broadcast([P, B * MT, C]),
                               ALU.mult).then_inc(mem_n_ok, 1)
            pool.wait_ge(mem_n_ok, 1)
            normalise(0, 0)
            normalise(0, 1)
            power(0, B)
            for b in range(1, B):
                normalise(b, 0)
                normalise(b, 1)
                power(b, B)
            for b in range(B):
                power(b, 2 * B)
            pool.wait_ge(slot_ok, 1)
            pool.wait_ge(filled, 16)
            for t in range(TT):
                pool.indirect_dma_start(
                    out=sorted_in, out_offset=bass.IndirectOffsetOnAxis(ap=slot[:, t:t + 1], axis=0),
                    in_=xn[:, t], in_offset=None).then_inc(scattered[t], 16)
            pool.wait_ge(y_out[0], 16 * ((BLOCKS + 1) // 2))
            pool.wait_ge(y_out[1], 16 * (BLOCKS // 2))
            for t in range(TT):
                pool.indirect_dma_start(
                    out=yg[:, t], out_offset=None, in_=sorted_out,
                    in_offset=bass.IndirectOffsetOnAxis(ap=slot[:, t:t + 1], axis=0)).then_inc(gathered[t], 16)

        @block.scalar
        def _(act):
            steps = [0]

            def chain(ins):
                steps[0] += 1
                ins.then_inc(act_step, 1)
                act.wait_ge(act_step, steps[0])

            act.wait_ge(c_in, W1)
            act.activation(bqk_s[:, 1:2], bqk[:, 1:2], ACT.Copy)
            chain(act.mul(bqk_s[:, 0:1], bqk[:, 0:1], SCALE))

            for b in range(B):
                act.wait_ge(xT_ps, b + 1)
                act.activation(xnT[:, NT * b:NT * b + NT, :], ps[:, 6 + b % 2, 0:N], ACT.Copy).then_inc(xT_ok, 1)
                act.wait_ge(qk_ps, b + 1)
                if b >= 2:
                    act.wait_ge(parts_ok, b - 1)
                for j, s in ((0, SCALE), (1, 1.0)):
                    src = s_ring[b % 2][:, N * j:N * j + N]
                    act.activation(qk_f[:, b % 2, j], src, ACT.Identity, bias=bqk_s[:, j:j + 1], scale=s)
                    last = act.activation(qk_parts[:, b, 0, j], src, ACT.Identity,
                                          bias=bqk_s[:, j:j + 1], scale=s)
                last.then_inc(qk_fok, 1)
                if b >= 1:
                    act.wait_ge(mem_in, 16)
                    for t in ((), range(0, 4), range(4, 9), range(9, B * MT))[b]:
                        last = act.activation(squares[:, t], mem[:, t], ACT.Square, accum_out=mem_ss[:, t:t + 1])
            last.then_inc(sq_ok, 1)
            act.wait_ge(sq_ok, 1)

            def max_copy(b):
                act.wait_ge(mT_ps, b + 1)
                rows, dst = (3 * H, max_t) if b < B else (3 * XH, xmax_t)
                if b % B >= 2:
                    act.wait_ge(max_out[b - 2], 16)
                act.activation(dst[:, b % 2], misc[0:rows, 0:P].bitcast(BF16), ACT.Copy).then_inc(mT_ok, 1)

            def exps(b, p):
                if b >= 1:
                    act.wait_ge(pv_ok, 2 * (b - 1) + p // 4 + 1)
                for i in range(2):
                    g = 2 * (PAIRS * b + p) + i
                    act.wait_ge(t_ready, g + 1)
                    act.activation(probs[:, p, 512 * i:512 * i + 512], t_ring[g % 3], ACT.Exp).then_inc(exp_ok, 1)

            def o_copy(b, g):
                act.wait_ge(pv_ok, 2 * b + g + 1)
                if b >= 1:
                    act.wait_ge(on_ok, 2 * (b - 1) + g + 1)
                    act.wait_ge(den_ps, 2 * (b - 1) + g + 1)
                act.activation(o_sb[:, g], o_ps[g][:, 0:N], ACT.Copy).then_inc(o_ok, 1)

            def cross_T(b):
                act.wait_ge(xT_ps, B + b + 1)
                act.activation(xnT[:, NT * b:NT * b + NT, :], misc[:, 0:N], ACT.Copy).then_inc(xT_ok, 1)

            max_copy(0)
            for i in range(4):
                act.wait_ge(memT_ps, i + 1)
                act.activation(memT[:, 4 * i:4 * i + 4, :], ps[:, 2 + i, :], ACT.Copy).then_inc(memT_ok, 1)
            act.wait_ge(kv_ps, 1)
            act.activation(xv_t[:], ps[:, 4, :], ACT.Copy).then_inc(xvt_ok, 1)
            act.wait_ge(xv_ps, 1)
            act.activation(xv[:], ps[:, 5, :], ACT.Copy).then_inc(xv_ok, 1)
            for b in range(B):
                for p in range(PAIRS):
                    exps(b, p)
                    if b >= 1 and p == 4:
                        o_copy(b - 1, 1)
                    if b >= 1 and p == 0:
                        o_copy(b - 1, 0)
                    if b >= 2 and p == 3:
                        cross_T(b - 2)
                    if p == 6:
                        max_copy(b + 1)
            o_copy(B - 1, 0)
            o_copy(B - 1, 1)

            def xexps(b, mt):
                slot = (MT * b + mt) % 8
                if MT * b + mt >= 8:
                    act.wait_ge(xpv_ok, MT * b + mt - 8 + 1)
                else:
                    act.wait_ge(pv_ok, 2 * B)
                for i in range(2):
                    g = B * H + 2 * (MT * b + mt) + i
                    act.wait_ge(t_ready, g + 1)
                    act.activation(probs[:, slot, 512 * i:512 * i + 512], t_ring[g % 3], ACT.Exp).then_inc(exp_ok, 1)

            for b in range(B):
                for mt in range(MT):
                    if (b, mt) == (0, 2):
                        max_copy(B + 1)
                    if (b, mt) == (2, 2):
                        max_copy(B + 3)
                    xexps(b, mt)
                    if b < 2 and mt == 0:
                        cross_T(b + 2)
                    if (b, mt) == (1, 2):
                        max_copy(B + 2)
            for b in range(B):
                act.wait_ge(xT3_ps, b + 1)
                act.activation(xnT[:, NT * b:NT * b + NT, :], ps[:, b, 0:N], ACT.Copy).then_inc(xT_ok, 1)

            def block_T(j):
                act.wait_ge(xsT_ps, j + 1)
                if j >= 2:
                    act.wait_ge(h_ps, j - 1)
                act.activation(xsT[:, j % 2], ps[:, j % 2, 0:P], ACT.Copy).then_inc(xsT_ok, 1)

            block_T(0)
            block_T(1)
            for j in range(BLOCKS):
                act.wait_ge(h_ok, j + 1)
                if j >= 2:
                    act.wait_ge(gT_ps, j - 1)
                act.activation(act_h[:, F * (j % 2):F * (j % 2) + F], hid[:, F * (j % 2):F * (j % 2) + F],
                               ACT.Gelu).then_inc(g_ok, 1)
                if j + 2 < BLOCKS:
                    block_T(j + 2)

        @block.vector
        def _(dve):
            steps = [0]

            def chain(ins):
                steps[0] += 1
                ins.then_inc(dve_step, 1)
                dve.wait_ge(dve_step, steps[0])

            def variance(b):
                for t in range(NT * b, NT * b + NT):
                    last = dve.bn_stats(stats[:, t], x[:, t])
                chain(last)
                for t in range(NT * b, NT * b + NT):
                    last = dve.bn_aggr(mv[:, t], stats[:, t])
                chain(last)
                dve.tensor_scalar(var_eps[:, NT * b:NT * b + NT], mv[:, NT * b:NT * b + NT, 1], LN_EPS, None,
                                  ALU.add).then_inc(var_ok, 1)

            def normal(b, first):
                dve.wait_ge(rstd_ok, first + b + 1)
                if first:
                    dve.wait_ge(xT_ps, first - B + b + 1)
                for t in range(NT * b, NT * b + NT):
                    last = dve.tensor_scalar(xn[:, t], x[:, t], mv[:, t, 0:1], rstd[:, t:t + 1],
                                             ALU.subtract, ALU.mult)
                last.then_inc(xn_ok, 1)

            def split(b):
                dve.wait_ge(qk_fok, b + 1)
                if b >= 1:
                    dve.wait_ge(parts_ok, b)
                whole = qk_f[:, b % 2].rearrange("p a n -> p (a n)")
                part = [qk_parts[:, b, s].rearrange("p a n -> p (a n)") for s in range(3)]
                chain(dve.tensor_tensor(qk_r[:], whole, part[0], ALU.subtract))
                chain(dve.tensor_copy(part[1], qk_r[:]))
                dve.tensor_tensor(part[2], qk_r[:], part[1], ALU.subtract).then_inc(parts_ok, 1)

            def values(b):
                dve.wait_ge(v_ps, b + 1)
                src = ps[:, 2 + b, 0:NT * P].rearrange("p (t i d) -> p t i d", i=2, d=D)
                bias = bv[:].rearrange("p a (t i d) -> p (a t) i d", i=2, d=D)
                for i in range(2):
                    last = dve.tensor_tensor(v_aug[:, b, :, i, D * i:D * i + D], src[:, :, i],
                                             bias[:, :, i], ALU.add)
                last.then_inc(v_ok, 1)

            dve.memset(q_st[:, 0].bitcast(F32), 0.0)
            dve.memset(k_bd[:, 0].bitcast(F32), 0.0).then_inc(k_zero, 1)
            for b in range(B):
                dve.wait_ge(x_in[b], 16)
                variance(b)
                if b >= 1:
                    normal(b - 1, 0)
            normal(B - 1, 0)
            for b in range(B):
                split(b)
                if b + 1 < B:
                    dve.memset(k_bd[:, b + 1].bitcast(F32), 0.0).then_inc(k_zero, 1)
            dve.wait_ge(c_in, W1)
            dve.tensor_copy(ident_b[:], ident[:]).then_inc(act_ident, 1)
            for b in range(B):
                dve.wait_ge(pool_const, 2 + b // 2)
                values(b)

            def maxima(g):
                b, c = divmod(g, CHUNKS)
                nt, pair = divmod(c, PAIRS)
                dve.wait_ge(s_ready, g + 1)
                if c == 0 and b >= 2:
                    dve.wait_ge(mparts_ok, b - 1)
                dve.tensor_reduce(neg_max[:, b % 2, nt, :, pair], s_ring[g % 2].rearrange("p (i m) -> p i m", i=2),
                                  AX.X, ALU.max, negate=True).then_inc(max_ok, 1)

            def split_max(b, whole, rest, parts, seen):
                dve.wait_ge(max_ok, seen)
                if b % B >= 1:
                    dve.wait_ge(mparts_ok, b)
                if b % B >= 2:
                    dve.wait_ge(mT_ps, b - 1)
                view = rest.rearrange("p (a h) -> p a h", a=NT)
                chain(dve.tensor_copy(parts[:, :, 0], whole))
                chain(dve.tensor_tensor(view, whole, parts[:, :, 0], ALU.subtract))
                chain(dve.tensor_copy(parts[:, :, 1], view))
                dve.tensor_tensor(parts[:, :, 2], view, parts[:, :, 1], ALU.subtract).then_inc(mparts_ok, 1)

            def max_split(b):
                split_max(b, neg_max[:, b % 2].rearrange("p a i r -> p a (i r)"), max_r[:], max_parts[:, b % 2],
                          CHUNKS * (b + 1))

            def context():
                dve.wait_ge(c2_in, W2)
                dve.scalar_tensor_tensor(xws[:], xw[:], rms_scale[:], xw[:], ALU.mult, ALU.add).then_inc(xws_ok, 1)
                chain(dve.tensor_copy(mask_f[:], mask_u8[:]))
                chain(dve.tensor_reduce(any_on[:], mask_f[:], AX.X, ALU.max))
                dve.tensor_scalar(mask_row[:], mask_f[:], any_on[:], -MASK_FILL, ALU.subtract, ALU.mult)
                dve.wait_ge(kv_ps, 1)
                dve.scalar_tensor_tensor(xk_t[:, 0], ps[:, 2, :], any_on[:], rope_k[:, 0], ALU.mult, ALU.mult)
                chain(dve.scalar_tensor_tensor(xk_t[:, 1], ps[:, 3, :], any_on[:], rope_k[:, 1], ALU.mult, ALU.mult))
                chain(dve.tensor_tensor(xk_t[:, 0], xk_t[:, 0], xk_t[:, 1], ALU.add))
                chain(dve.tensor_copy(xk_parts[:, 0], xk_t[:, 0]))
                chain(dve.tensor_tensor(xk_t[:, 1], xk_t[:, 0], xk_parts[:, 0], ALU.subtract))
                chain(dve.tensor_copy(xk_parts[:, 1], xk_t[:, 1]))
                dve.tensor_tensor(xk_parts[:, 2], xk_t[:, 1], xk_parts[:, 1], ALU.subtract).then_inc(xk_ok, 1)

            def reciprocals(b, g):
                dve.wait_ge(den_ps, 2 * b + g + 1)
                if b >= 1:
                    dve.wait_ge(on_ok, 2 * (b - 1) + g + 1)
                dve.reciprocal(rec[:, g], misc[:, 0:N]).then_inc(rec_ok, 1)

            def residual(b, first):
                dve.wait_ge(proj_ps, first + b + 1)
                t = x[:, NT * b:NT * b + NT, :]
                dve.tensor_tensor(t, t, misc[:, 0:N].rearrange("p (a n) -> p a n", a=NT), ALU.add).then_inc(x_ok, 1)
                dve.wait_ge(x_ok, first + b + 1)

            def cross_q(b):
                dve.wait_ge(xq_ps, b + 1)
                if b == 0:
                    dve.wait_ge(c3_in, W3)
                if b >= 1:
                    dve.wait_ge(xq_ok, b)
                if b >= 2:
                    dve.wait_ge(xq_out[b - 2], 16)
                dve.tensor_tensor(xq_t[:, 0], misc[:, 0:N], rope_q[:, 0], ALU.mult)
                dve.tensor_tensor(xq_t[:, 1], misc[:, N:2 * N], rope_q[:, 1], ALU.mult).then_inc(xrope_ok, 1)
                dve.wait_ge(xrope_ok, b + 1)
                part = [xq_parts[:, b % 2, s] for s in range(3)]
                chain(dve.tensor_tensor(xq_t[:, 0], xq_t[:, 0], xq_t[:, 1], ALU.add))
                chain(dve.tensor_copy(part[0], xq_t[:, 0]))
                chain(dve.tensor_tensor(xq_t[:, 1], xq_t[:, 0], part[0], ALU.subtract))
                chain(dve.tensor_copy(part[1], xq_t[:, 1]))
                dve.tensor_tensor(part[2], xq_t[:, 1], part[1], ALU.subtract).then_inc(xq_ok, 1)

            def xmaxima(g):
                b, c = divmod(g, XCHUNKS)
                nt, h = divmod(c, XH)
                g += B * CHUNKS
                dve.wait_ge(s_ready, g + 1)
                if c == 0 and b >= 2:
                    dve.wait_ge(mparts_ok, B + b - 1)
                dve.tensor_reduce(xneg_max[:, b % 2, nt, h:h + 1], s_ring[g % 2], AX.X, ALU.max,
                                  negate=True).then_inc(max_ok, 1)
                if c == XCHUNKS - 1:
                    split_max(B + b, xneg_max[:, b % 2], xmax_r[:], xmax_parts[:, b % 2],
                              B * CHUNKS + XCHUNKS * (b + 1))

            def next_maxima(g):
                maxima(g)
                if g % CHUNKS == CHUNKS - 1:
                    max_split(g // CHUNKS)

            for g in range(CHUNKS + 2):
                next_maxima(g)
            context()
            for g in range(CHUNKS + 2, CHUNKS + LEAD):
                next_maxima(g)
            for b in range(B):
                for p in range(PAIRS):
                    if b >= 2 and p == 0:
                        normal(b - 2, B)
                    for g in range(CHUNKS + LEAD + 2 * (PAIRS * b + p), CHUNKS + LEAD + 2 * (PAIRS * b + p) + 2):
                        if g < B * CHUNKS:
                            next_maxima(g)
                    if b == B - 1 and p not in (4, 5):
                        for g in range(2 * p - 4 * (p > 5), 2 * p - 4 * (p > 5) + 2):
                            xmaxima(g)
                    if b >= 1 and p == 1:
                        reciprocals(b - 1, 0)
                    if b >= 2 and p == 3:
                        cross_q(b - 2)
                    if b >= 1 and p == 5:
                        reciprocals(b - 1, 1)
                    if b >= 1 and p == 7:
                        residual(b - 1, 0)
                        variance(b - 1)
            normal(B - 2, B)
            for g in range(12, 16):
                xmaxima(g)
            reciprocals(B - 1, 0)

            def xnormalise(b):
                dve.wait_ge(xpv_ok, MT * (b + 1))
                dve.wait_ge(proj_ps, B + b)
                chain(dve.reciprocal(rec[:, 0], o_ps[b % 2][:, N:2 * N]))
                dve.tensor_tensor(o_n[:, 0], o_ps[b % 2][:, 0:N], rec[:, 0], ALU.mult).then_inc(xon_ok, 1)

            for b in range(B):
                for mt in range(MT):
                    for g in XAHEAD.get((b, mt), ()):
                        xmaxima(g)
                    if (b, mt) == (0, 1):
                        cross_q(2)
                    if (b, mt) == (0, 2):
                        reciprocals(B - 1, 1)
                    if (b, mt) == (0, 3):
                        residual(B - 1, 0)
                        variance(B - 1)
                    if (b, mt) == (1, 0):
                        normal(B - 1, B)
                    if b >= 1 and mt == 0:
                        xnormalise(b - 1)
                    if (b, mt) == (1, 1):
                        cross_q(3)
                    if b >= 1 and mt == (0, 3, 2, 1)[b]:
                        residual(b - 1, B)
                        variance(b - 1)
                    if (b, mt) in ((2, 0), (2, 3), (3, 2)):
                        normal(((2, 0), (2, 3), (3, 2)).index((b, mt)), 2 * B)
            xnormalise(B - 1)
            residual(B - 1, B)
            variance(B - 1)
            normal(B - 1, 2 * B)

            table = [route_c[:, 64 * i:64 * i + 64].rearrange("p (a e) -> p a e", e=E) for i in range(3)]
            rank_down, steps128, before = table
            block_no = route_c[:, 192:192 + BLOCKS * E].rearrange("p (j e) -> p j e", e=E)
            dve.wait_ge(route_in, 5 * 16)
            dve.wait_ge(score_ps, 1)
            chain(dve.tensor_tensor(sc[:], ps[:, 7, 0:TT * E].rearrange("p (t e) -> p t e", e=E),
                                    br[:].unsqueeze(1).to_broadcast([P, TT, E]), ALU.add))
            chain(dve.tensor_reduce(top[:, 0], sc[:], AX.X, ALU.max))
            chain(dve.tensor_tensor(cand[:], sc[:], top[:, 0].unsqueeze(2).to_broadcast([P, TT, E]), ALU.is_ge))
            chain(dve.tensor_tensor(cand[:], cand[:], rank_down, ALU.mult))
            chain(dve.tensor_reduce(top[:, 1], cand[:], AX.X, ALU.max))
            dve.tensor_tensor(one_hot[:], cand[:], top[:, 1].unsqueeze(2).to_broadcast([P, TT, E]),
                              ALU.is_equal).then_inc(hot_ok, 1)
            dve.wait_ge(rank_ps, 1)
            rank = ps[:, 0, 0:TT * E].rearrange("p (t e) -> p t e", e=E)
            chain(dve.tensor_tensor(sc[:], ps[:, 0, TT * E:TT * E + E].unsqueeze(2).to_broadcast([P, E, TT]),
                                    steps128, ALU.is_gt))
            chain(dve.tensor_reduce(blk[:, 0], sc[:], AX.X, ALU.add))
            chain(dve.tensor_tensor(sc[:], blk[:, 0].unsqueeze(1).to_broadcast([P, E, E]), before, ALU.mult))
            chain(dve.tensor_reduce(blk[:, 1], sc[:], AX.X, ALU.add))
            chain(dve.scalar_tensor_tensor(cand[:], blk[:, 1].unsqueeze(1).to_broadcast([P, TT, E]), float(P),
                                           rank, ALU.mult, ALU.add))
            chain(dve.tensor_tensor(cand[:], cand[:], one_hot[:], ALU.mult))
            chain(dve.tensor_reduce(slot_f[:], cand[:], AX.X, ALU.add))
            dve.tensor_copy(slot[:], slot_f[:]).then_inc(slot_ok, 1)
            chain(dve.tensor_tensor(blk[:, 2], blk[:, 0], blk[:, 1], ALU.add))
            chain(dve.tensor_tensor(blk_t[:], blk[:, 2].unsqueeze(1).to_broadcast([P, BLOCKS, E]), block_no,
                                    ALU.is_le))
            chain(dve.tensor_reduce(blk_f[:], blk_t[:], AX.X, ALU.add))
            dve.tensor_scalar(block_expert[:], blk_f[:], float(E - 1), None, ALU.min).then_inc(table_ok, 1)
            dve.wait_ge(table_ok, 1)
            dve.wait_ge(ffn_in, 4 * 16)

            def hidden(j):
                e = dve.value_load(block_expert[0:1, j:j + 1], min_val=0, max_val=E - 1)
                dve.wait_ge(h_ps, j + 1)
                if j >= 2:
                    dve.wait_ge(g_ok, j - 1)
                dve.tensor_tensor(hid[:, F * (j % 2):F * (j % 2) + F], ps[:, 2 + j % 2, :],
                                  b1[:, bass.ds(e * F, F)], ALU.add).then_inc(h_ok, 1)

            def hidden_T(j):
                dve.wait_ge(gT_ps, j + 1)
                if j >= 2:
                    dve.wait_ge(y_ps, j - 1)
                dve.tensor_copy(act_T[:, F * (j % 2):F * (j % 2) + F], ps[:, 4 + j % 2, :]).then_inc(gT_ok, 1)

            def block_out(j):
                e = dve.value_load(block_expert[0:1, j:j + 1], min_val=0, max_val=E - 1)
                dve.wait_ge(y_ps, j + 1)
                if j >= 2:
                    dve.wait_ge(y_out[j % 2], 16 * (j // 2))
                dve.tensor_tensor(ys[:, C * (j % 2):C * (j % 2) + C], ps[:, 6 + j % 2, 0:C],
                                  b2[:, bass.ds(e * C, C)], ALU.add).then_inc(y_ok, 1)

            hidden(0)
            for j in range(BLOCKS):
                if j + 1 < BLOCKS:
                    hidden(j + 1)
                hidden_T(j)
                if j >= 1:
                    block_out(j - 1)
            block_out(BLOCKS - 1)
            for b in range(B):
                for t in range(NT):
                    dve.wait_ge(gathered[NT * b + t], 16)
                t = x[:, NT * b:NT * b + NT]
                dve.tensor_tensor(t, t, yg[:, NT * b:NT * b + NT], ALU.add).then_inc(x_ok, 1)

        @block.tensor
        def _(pe):
            mm = nc.tensor.matmul

            def transposes(b, first, half):
                pe.wait_ge(xn_ok, first + b + 1)
                for t in range(NT):
                    last = nc.tensor.transpose(half[:, P * t:P * t + P], xn[:, NT * b + t], ident[:])
                last.then_inc(xT_ps, 1)

            def project(b):
                pe.wait_ge(xT_ok, b + 1)
                if b >= 2:
                    pe.wait_ge(qk_fok, b - 1)
                rhs = xnT[:, NT * b:NT * b + NT, :].rearrange("p t n -> p (t n)")
                for j in range(2):
                    last = mm(s_ring[b % 2][:, N * j:N * j + N], wqk[:, j], rhs, start=True, stop=True)
                last.then_inc(qk_ps, 1)
                for t in range(NT):
                    last = mm(ps[:, 2 + b, P * t:P * t + P], xnT[:, NT * b + t], wv[:], start=True, stop=True)
                last.then_inc(v_ps, 1)

            pe.wait_ge(c_in, W1)
            transposes(0, 0, ps[:, 6, :])
            for b in range(B):
                if b + 1 < B:
                    if b >= 1:
                        pe.wait_ge(xT_ok, b)
                    transposes(b + 1, 0, ps[:, 6 + (b + 1) % 2, :])
                project(b)

            def scores(g):
                b, c = divmod(g, CHUNKS)
                nt, pair = divmod(c, PAIRS)
                if c == 0:
                    pe.wait_ge(stacked[b], 12 * 16)
                if g == 0:
                    pe.wait_ge(qk_fok, B)
                if g >= 2:
                    pe.wait_ge(max_ok, g - 1)
                mm(s_ring[g % 2], q_st[:, b, pair, P * nt:P * nt + P],
                   k_bd[:, b, :, pair], start=True, stop=True).then_inc(s_ready, 1)

            def max_transposes(b):
                pe.wait_ge(mparts_ok, b + 1)
                if b == 0:
                    pe.wait_ge(xT_ok, B)
                    pe.wait_ge(act_ident, 1)
                elif b == 1:
                    pe.wait_ge(mT_ok, 1)
                elif b <= B:
                    pe.wait_ge(rec_ok, 2 * b - 2)
                elif b < B + 3:
                    pe.wait_ge(xrope_ok, b - B + 2)
                else:
                    pe.wait_ge(x_ok, B + 1)
                rows, src = (3 * H, max_parts) if b < B else (3 * XH, xmax_parts)
                for nt in range(NT):
                    last = nc.tensor.transpose(misc[0:rows, 64 * nt:64 * nt + 64].bitcast(BF16),
                                               src[:, b % 2, nt].rearrange("p s h -> p (s h)"), ident_b[:])
                last.then_inc(mT_ps, 1)

            def context():
                pe.wait_ge(mem_n_ok, 1)
                pe.wait_ge(v_ok, B)
                for t in range(B * MT):
                    last = nc.tensor.transpose(ps[:, 2 + t // 4, P * (t % 4):P * (t % 4) + P], mem[:, t], ident[:])
                    if t % 4 == 3:
                        last.then_inc(memT_ps, 1)
                pe.wait_ge(memT_ok, 4)
                pe.wait_ge(xws_ok, 1)
                for j in range(3):
                    w = xws[:, 2 * P + XD * j:2 * P + XD * j + XD]
                    for b in range(B):
                        last = mm(ps[XD * b:XD * b + XD, 2 + j, :], w,
                                  memT[:, MT * b:MT * b + MT, :].rearrange("p t n -> p (t n)"),
                                  start=True, stop=True)
                last.then_inc(kv_ps, 1)
                pe.wait_ge(xvt_ok, 1)
                for t in range(MT):
                    last = nc.tensor.transpose(ps[:, 5, P * t:P * t + P], xv_t[:, P * t:P * t + P], ident[:])
                last.then_inc(xv_ps, 1)

            def weights(b, p):
                if p == 0:
                    pe.wait_ge(max_in[b], 2 * 16)
                if b == 0 and p == 0:
                    pe.wait_ge(xk_ok, 1)
                    pe.wait_ge(xv_ok, 1)
                for i in range(2):
                    g = 2 * (PAIRS * b + p) + i
                    if g >= 3:
                        pe.wait_ge(exp_ok, g - 2)
                    for mt in range(NT):
                        last = mm(t_ring[g % 3][:, N * mt:N * mt + N], k_bd[:, b, i, p, P * mt:P * mt + P],
                                  q_st[:, b, p], start=True, stop=True)
                    last.then_inc(t_ready, 1)

            def attend(b, g, r):
                i, mt = divmod(r, NT)
                if r == 0:
                    pe.wait_ge(exp_ok, 2 * (PAIRS * b + 4 * g + 4))
                    if b >= 1:
                        pe.wait_ge(o_ok, 2 * (b - 1) + g + 1)
                for q in range(4):
                    p = 4 * g + q
                    last = mm(o_ps[g][32 * q:32 * q + 32, 0:N], v_aug[:, b, PAIRS * mt + p, i],
                              probs[:, p, 512 * i + N * mt:512 * i + N * mt + N], start=(r == 0), stop=(r == 3))
                if r == 3:
                    last.then_inc(pv_ok, 1)

            def spread_sums(b, g):
                pe.wait_ge(o_ok, 2 * b + g + 1)
                if g == 0 and b == 0:
                    pe.wait_ge(mT_ok, 2)
                elif g == 0:
                    pe.wait_ge(x_ok, b)
                elif b == 0:
                    pe.wait_ge(rec_ok, 1)
                else:
                    pe.wait_ge(xrope_ok, b)
                if b == B - 1 and g == 1:
                    pe.wait_ge(mT_ok, B + 2)
                mm(misc[:, 0:N], spread[:], o_sb[:, g], start=True, stop=True).then_inc(den_ps, 1)

            def output(b):
                pe.wait_ge(on_ok, 2 * b + 2)
                if b == 0:
                    pe.wait_ge(c3_in, W3)
                pe.wait_ge(mT_ok, b + 3)
                for nt in range(NT):
                    for g in range(2):
                        last = mm(misc[:, P * nt:P * nt + P], o_n[:, g, P * nt:P * nt + P], wproj[:, g],
                                  start=(g == 0), stop=(g == 1))
                last.then_inc(proj_ps, 1)

            def cross_T(b):
                pe.wait_ge(rec_ok, min(2 * b + 3, 2 * B))
                transposes(b, B, misc)

            def cross_project(b):
                pe.wait_ge(xT_ok, B + b + 1)
                rhs = xnT[:, NT * b:NT * b + NT, :].rearrange("p t n -> p (t n)")
                for j in range(2):
                    last = mm(misc[:, N * j:N * j + N], xws[:, P * j:P * j + P], rhs, start=True, stop=True)
                last.then_inc(xq_ps, 1)

            def xscores(g):
                b, c = divmod(g, XCHUNKS)
                nt, h = divmod(c, XH)
                g += B * CHUNKS
                if c == 0:
                    pe.wait_ge(xq_in[b], 3 * 16)
                if b == 0 and c == 0:
                    pe.wait_ge(xk_in, 7 * 16)
                    pe.wait_ge(pool_const, 4)
                pe.wait_ge(max_ok, g - 1)
                mm(s_ring[g % 2], qx[0][0:96, b, h, P * nt:P * nt + P], kx[0][0:96, b], start=True, stop=False)
                mm(s_ring[g % 2], qx[1][0:97, b, h, P * nt:P * nt + P], kx[1][0:97, b],
                   start=False, stop=True).then_inc(s_ready, 1)

            for g in range(CHUNKS + 2):
                scores(g)
            max_transposes(0)
            context()
            for g in range(CHUNKS + 2, CHUNKS + LEAD):
                scores(g)
            for b in range(B):
                for p in range(PAIRS):
                    weights(b, p)
                    if p < 4 and b >= 1:
                        attend(b - 1, 1, p)
                    if p >= 4:
                        attend(b, 0, p - 4)
                    for g in range(CHUNKS + LEAD + 2 * (PAIRS * b + p), CHUNKS + LEAD + 2 * (PAIRS * b + p) + 2):
                        if g < B * CHUNKS:
                            scores(g)
                    if b == B - 1 and p not in (4, 5):
                        for g in range(2 * p - 4 * (p > 5), 2 * p - 4 * (p > 5) + 2):
                            xscores(g)
                    if p == 0 and b >= 1:
                        spread_sums(b - 1, 0)
                    if p == 2 and b >= 2:
                        cross_T(b - 2)
                    if p == 3 and b >= 2:
                        cross_project(b - 2)
                    if p == 5 and b >= 1:
                        spread_sums(b - 1, 1)
                    if p == 6:
                        max_transposes(b + 1)
                    if p == 7 and b >= 1:
                        output(b - 1)
            for p in range(4):
                attend(B - 1, 1, p)
                xscores(12 + p)
            spread_sums(B - 1, 0)

            def xweights(b, mt):
                if mt == 0:
                    pe.wait_ge(max_in[B + b], 16)
                for pair in range(2):
                    g = B * H + 2 * (MT * b + mt) + pair
                    pe.wait_ge(exp_ok, g - 2)
                    for j, rows in ((0, 99), (1, 97)):
                        last = mm(t_ring[g % 3], kx[j][0:rows, b, P * mt:P * mt + P],
                                  qx[j][0:rows, b, 2 * pair:2 * pair + 2].rearrange("p h n -> p (h n)"),
                                  start=(j == 0), stop=(j == 1))
                    last.then_inc(t_ready, 1)

            def xattend(b, mt):
                g = MT * b + mt
                pe.wait_ge(exp_ok, B * H + 2 * (g + 1))
                if mt == 0 and b < 2:
                    pe.wait_ge(o_ok, 2 * B - 1 + b)
                elif mt == 0:
                    pe.wait_ge(xon_ok, b - 1)
                for what in range(2):
                    for h in range(XH):
                        last = mm(o_ps[b % 2][32 * h:32 * h + 32, N * what:N * what + N],
                                  ones[:] if what else xv[:, mt, b], probs[:, g % 8, N * h:N * h + N],
                                  start=(mt == 0 and what == 0), stop=(mt == MT - 1), skip_group_check=True)
                last.then_inc(xpv_ok, 1)

            def xoutput(b):
                pe.wait_ge(xon_ok, b + 1)
                pe.wait_ge(mT_ok, min(B + b + 3, 2 * B))
                if b >= 2:
                    pe.wait_ge(x_ok, B + b)
                for nt in range(NT):
                    last = mm(misc[:, P * nt:P * nt + P], o_n[:, 0, P * nt:P * nt + P], wout[:],
                              start=True, stop=True)
                last.then_inc(proj_ps, 1)

            for b in range(B):
                for mt in range(MT):
                    if (b, mt) == (0, 2):
                        max_transposes(B + 1)
                    if (b, mt) == (2, 2):
                        max_transposes(B + 3)
                    xweights(b, mt)
                    if mt or b:
                        g = MT * b + mt - 1
                        xattend(g // MT, g % MT)
                    for g in XAHEAD.get((b, mt), ()):
                        xscores(g)
                    if (b, mt) in ((0, 0), (1, 0)):
                        cross_T(b + 2)
                    if (b, mt) in ((0, 1), (1, 1)):
                        cross_project(b + 2)
                    if (b, mt) == (0, 2):
                        spread_sums(B - 1, 1)
                    if (b, mt) == (0, 3):
                        output(B - 1)
                    if (b, mt) == (1, 2):
                        max_transposes(B + 2)
                    if b >= 1 and mt == (0, 3, 2, 1)[b]:
                        xoutput(b - 1)
            xattend(B - 1, MT - 1)
            xoutput(B - 1)

            pe.wait_ge(max_ok, B * (CHUNKS + XCHUNKS))
            pe.wait_ge(exp_ok, B * (H + 2 * MT))
            for b in range(B):
                pe.wait_ge(xn_ok, 2 * B + b + 1)
                for t in range(NT):
                    last = nc.tensor.transpose(ps[:, b, P * t:P * t + P], xn[:, NT * b + t], ident[:])
                last.then_inc(xT3_ps, 1)
            pe.wait_ge(route_in, 5 * 16)
            pe.wait_ge(x_ok, 2 * B)
            for b in range(B):
                pe.wait_ge(xT_ok, 2 * B + b + 1)
                for t in range(NT * b, NT * b + NT):
                    last = mm(ps[:, 7, E * t:E * t + E], xnT[:, t], wr[:], start=True, stop=True)
            last.then_inc(score_ps, 1)
            pe.wait_ge(hot_ok, 1)
            hot = one_hot[:].rearrange("p t e -> p (t e)")
            mm(ps[:, 0, 0:TT * E], tri[:], hot, start=True, stop=False, skip_group_check=True)
            for t in range(TT):
                last = mm(ps[:, 0, E * (t + 1):E * (TT + 1)].rearrange("p (a e) -> p a e", e=E), ones_b[:],
                          one_hot[:, t:t + 1].to_broadcast([P, TT - t, E]), start=False, stop=(t == TT - 1),
                          skip_group_check=True)
            last.then_inc(rank_ps, 1)

            def block_T(j):
                if j % (BLOCKS // 3) == 0:
                    pe.wait_ge(xs_in[j // (BLOCKS // 3)], 16)
                if j >= 2:
                    pe.wait_ge(xsT_ok, j - 1)
                nc.tensor.transpose(ps[:, j % 2, 0:P], xs[:, j], ident[:]).then_inc(xsT_ps, 1)

            def block_h(j):
                e = pe.value_load(block_expert[0:1, j:j + 1], min_val=0, max_val=E - 1)
                pe.wait_ge(xsT_ok, j + 1)
                if j >= 2:
                    pe.wait_ge(h_ok, j - 1)
                mm(ps[:, 2 + j % 2, :], xsT[:, j % 2], w1[:, bass.ds(e * F, F)], start=True,
                   stop=True).then_inc(h_ps, 1)

            def hidden_T(j):
                pe.wait_ge(g_ok, j + 1)
                if j >= 2:
                    pe.wait_ge(gT_ok, j - 1)
                for f in range(FT):
                    last = nc.tensor.transpose(ps[:, 4 + j % 2, P * f:P * f + P],
                                               act_h[:, F * (j % 2) + P * f:F * (j % 2) + P * f + P], ident[:])
                last.then_inc(gT_ps, 1)

            def block_y(j):
                e = pe.value_load(block_expert[0:1, j:j + 1], min_val=0, max_val=E - 1)
                pe.wait_ge(gT_ok, j + 1)
                if j >= 2:
                    pe.wait_ge(y_ok, j - 1)
                for f in range(FT):
                    last = mm(ps[:, 6 + j % 2, 0:C], act_T[:, F * (j % 2) + P * f:F * (j % 2) + P * f + P],
                              w2[:, bass.ds(e * F + f * C, C)], start=(f == 0), stop=(f == FT - 1))
                last.then_inc(y_ps, 1)

            pe.wait_ge(table_ok, 1)
            pe.wait_ge(ffn_in, 4 * 16)
            block_T(0)
            block_T(1)
            block_h(0)
            for j in range(BLOCKS):
                if j + 1 < BLOCKS:
                    block_h(j + 1)
                if j + 2 < BLOCKS:
                    block_T(j + 2)
                hidden_T(j)
                if j >= 1:
                    block_y(j - 1)
            block_y(BLOCKS - 1)


def layout(inputs):
    i = {k: np.asarray(v) for k, v in inputs.items()}
    order = np.arange(C).reshape(PAIRS, 2, D).transpose(2, 1, 0).reshape(-1)
    wqkv, bqkv = i["L0_attn_w_qkv"], i["L0_attn_b_qkv"]
    wqk = np.stack([wqkv[0:C].T[:, order], wqkv[C:2 * C].T[:, order]], 1)
    bqk = np.stack([bqkv[0:C][order], bqkv[C:2 * C][order]], 1)
    wproj = np.zeros((P, 2, C), np.float32)
    spread = np.zeros((P, P), np.float32)
    for g in range(2):
        for q in range(4):
            for j in range(2):
                h = 2 * (4 * g + q) + j
                wproj[32 * q + D * j:32 * q + D * j + D, g] = i["L0_attn_w_proj"].T[h * D:h * D + D]
    for q in range(4):
        spread[32 * q + 16, 32 * q:32 * q + 32] = 1
        spread[32 * q + 16, 32 * q + D:32 * q + 2 * D] = 0
        spread[32 * q + 17, 32 * q + D:32 * q + 2 * D] = 1
    wproj[16, 0] = i["L0_attn_b_proj"]
    swap = (np.arange(XD) + XD // 2) % XD
    wq = i["L0_xattn_q_w"].transpose(1, 2, 0)
    wk, wv = i["L0_xattn_kv_w"][0, 0], i["L0_xattn_kv_w"][1, 0]
    xw = np.concatenate([wq.reshape(C, -1), wq[:, swap].reshape(C, -1), wk, wk[:, swap], wv], 1)
    freq = (np.float32(10000.0) ** (np.float32(2.0 / XD) * np.arange(XD // 2, dtype=np.float32))).astype(np.float32)

    def rope(positions, scale):
        angle = positions.astype(np.float32)[None, :] / freq[:, None]
        cos, sin = np.cos(angle), np.sin(angle)
        t = np.stack([np.concatenate([cos, cos]), np.concatenate([-sin, sin])], 1) * np.float32(scale)
        return t.astype(np.float32)

    a = {
        "x": i["x"].reshape(B, NT, P, C).transpose(0, 2, 1, 3),
        "ident": np.eye(P, dtype=np.float32),
        "wqk": wqk, "bqk": bqk, "wv": wqkv[2 * C:].T,
        "bv": np.broadcast_to(bqkv[2 * C:], (P, NT, C)),
        "wproj": wproj, "spread": spread,
        "mem": i["ctx_1024"].reshape(B * MT, P, C).transpose(1, 0, 2),
        "mask": np.repeat(i["mask_BxS2_bk0"], XD, axis=0),
        "rms_scale": i["L0_xattn_rms_scale"].reshape(C, 1),
        "xw": xw, "wout": i["L0_xattn_out_w"].reshape(XH * XD, C),
        "rope_q": np.repeat(rope(np.arange(M, M + N), XD ** -0.5), XH, axis=0),
        "rope_k": np.tile(rope(np.arange(M), 1.0), (B, 1, 1)),
    }
    w1, w2 = i["L0_ffn_w1"], i["L0_ffn_w2"]
    t, e = np.arange(TT), np.arange(E)
    route = np.concatenate([
        np.tile(E - e, TT), np.tile(P * t, E), (e[None, :] < e[:, None]).reshape(-1), np.repeat(np.arange(BLOCKS), E)])
    a.update({
        "zeros": np.zeros((SLOTS, C), np.float32),
        "w1": w1.transpose(1, 0, 2).reshape(P, E * F),
        "w2": w2.reshape(E, FT, P, C).transpose(2, 0, 1, 3).reshape(P, E * F),
        "b1": np.broadcast_to(i["L0_ffn_b1"].reshape(-1), (P, E * F)),
        "b2": np.broadcast_to(i["L0_ffn_b2"].reshape(-1), (P, E * C)),
        "wr": i["L0_ffn_wr"],
        "br": np.broadcast_to(i["L0_ffn_br"], (P, E)),
        "route_c": np.broadcast_to(route.astype(np.float32), (P, route.size)),
        "tri": np.triu(np.ones((P, P)), 1).astype(mybir.dt.np(BF16)),
        "ones_b": np.ones((P, P), mybir.dt.np(BF16)),
    })
    return {k: np.ascontiguousarray(v) for k, v in a.items()}


def kernel(**inputs):
    import concourse.bacc as bacc
    from concourse.bass_utils import run_bass_kernel_spmd

    nc = bacc.Bacc("TRN2", target_bir_lowering=False, num_devices=1)
    arrays = layout(inputs)
    a = {k: nc.dram_tensor("in_" + k, v.shape, mybir.dt.from_np(v.dtype), kind="ExternalInput").ap()
         for k, v in arrays.items()}
    a["out"] = nc.dram_tensor("out", (B, P, NT, C), F32, kind="ExternalOutput").ap()
    build(nc, a)
    r = run_bass_kernel_spmd(nc, [{"in_" + k: v for k, v in arrays.items()}], core_ids=[0])
    y = r.results[0]["out"].reshape(B, P, NT, C).transpose(0, 2, 1, 3).reshape(B, N, C)
    return np.ascontiguousarray(y)
```

```python
from contextlib import ExitStack

import concourse.bass as bass
import concourse.mybir as mybir
import numpy as np

F32 = mybir.dt.float32
BF16 = mybir.dt.bfloat16
I32 = mybir.dt.int32
U8 = mybir.dt.uint8
ALU = mybir.AluOpType
ACT = mybir.ActivationFunctionType
AX = mybir.AxisListType

B, N, C = 4, 256, 128
H, D = 16, 8
M = 512
XH, XD = 4, 32
E, F = 8, 512
P = 128
NT = N // P
TT = B * NT
MT = M // P
PAIRS = H // 2
CHUNKS = NT * PAIRS
XCHUNKS = NT * XH
LEAD = 8
XFIRST = ((0, 1), (2, 3), (4, 5), (6, 7), (), (), (), (), (), (8,), (9, 10), (11, 12))
XAHEAD = {(0, 0): range(13, 16), (1, 0): range(16, 20), (1, 1): range(20, 24), (2, 0): range(24, 28), (2, 1): range(28, 32)}
SCALE = D ** -0.5
LN_EPS = 1e-5
RMS_EPS = 1e-6
MASK_FILL = -2.3819763e38
FT = F // P
BLOCKS = TT + E - 1
SLOTS = BLOCKS * P
ROW_W = 2 * C + 1
XS_LOADS = ((0, 1), (1, 4), (5, BLOCKS - 5))
Y_BUFS = 8

ROW = (0, 8, 16, 24, 40, 48)
MAX_ROW = 32
Q_COPIES = ((ROW[0], 3, 0), (ROW[3], 1, 0), (ROW[4], 2, 0))
K_COPIES = ((ROW[0], 3, 0), (ROW[3], 1, 2), (ROW[4], 2, 1))
XQ_COPIES = ((0, 0, 3, 0), (1, 0, 2, 0), (1, 2 * XD, 1, 0))
XK_COPIES = ((0, 0, 3, 0), (1, 0, 2, 1), (1, 2 * XD, 1, 2))
XMAX_ROW = 96
ONE_ONE = 0x3F803F80


def build(nc, a):
    ctx = ExitStack()
    with ctx:
        def sb(name, shape, dt=F32):
            return ctx.enter_context(nc.sbuf_tensor(name, shape, dt))

        def sem(name):
            return ctx.enter_context(nc.semaphore(name))

        qk_scratch = nc.dram_tensor("qk_scratch", [B, 3, 2, P, N], BF16).ap()
        max_scratch = nc.dram_tensor("max_scratch", [B, 3, 2, PAIRS, N], BF16).ap()
        xmax_scratch = nc.dram_tensor("xmax_scratch", [B, 3, XH, N], BF16).ap()
        mask_scratch = nc.dram_tensor("mask_scratch", [B, M], BF16).ap()
        xq_scratch = nc.dram_tensor("xq_scratch", [B, 3, P, N], BF16).ap()
        xk_scratch = nc.dram_tensor("xk_scratch", [P, 3, M], BF16).ap()
        sorted_in = nc.dram_tensor("sorted_in", [SLOTS, ROW_W], F32).ap()

        rows = sb("rows", [P, TT, ROW_W])
        xn = rows[:, :, 0:C]
        x = rows[:, :, C:2 * C]
        row_id = rows[:, :, 2 * C].bitcast(I32)
        warm = sb("warm", [P, 1])
        b1_e = sb("b1_e", [P, 2, FT])
        row_ids = sb("row_ids", [P, TT], I32)
        xnT = sb("xnT", [P, TT, P])
        stats = sb("stats", [P, TT, 6])
        mv = sb("mv", [P, TT, 2])
        var_eps = sb("var_eps", [P, TT])
        rstd = sb("rstd", [P, TT])
        w2nd = sb("w2nd", [P, TT])
        half = sb("half", [P, 16])
        ident = sb("ident", [P, P])
        ident_b = sb("ident_b", [P, P], BF16)
        wqk = sb("wqk", [P, 2, P])
        wv = sb("wv", [P, P])
        bqk = sb("bqk", [P, 2])
        bqk_s = sb("bqk_s", [P, 2])
        bv = sb("bv", [P, NT, P])
        wproj = sb("wproj", [P, P])
        bproj = sb("bproj", [1, C])
        qk_f = sb("qk_f", [P, 2, 2, N])
        qk_r = sb("qk_r", [P, 2 * N])
        qk_parts = sb("qk_parts", [P, B, 3, 2, N], BF16)
        q_st = sb("q_st", [P, B, PAIRS, N], BF16)
        k_bd = sb("k_bd", [P, B, 2, PAIRS, N], BF16)
        v_aug = sb("v_aug", [P, B, NT * PAIRS, 2, 32])
        probs = sb("probs", [P, 8, 1024])
        neg_max = sb("neg_max", [P, 2, NT, 2, PAIRS])
        max_r = sb("max_r", [P, NT * H])
        max_parts = sb("max_parts", [P, 2, NT, 3, H], BF16)
        max_t = sb("max_t", [3 * H, 2, N], BF16)
        o_sb = sb("o_sb", [P, 2, N])
        rec = sb("rec", [P, N])
        o_n = sb("o_n", [P, N])
        o_nT = sb("o_nT", [P, N])
        mem = sb("mem", [P, B * MT, C])
        memT = probs[:, 6:8, :].rearrange("p s (t n) -> p (s t) n", n=P)
        mem_ss = sb("mem_ss", [P, B * MT])
        mem_rs = sb("mem_rs", [P, B * MT])
        squares = probs[:, 4:6, :].rearrange("p s (t n) -> p (s t) n", n=P)
        b2 = mem[:].rearrange("p t c -> p (t c)")[:, 0:E * C]
        rms_scale = sb("rms_scale", [P, 1])
        xw = sb("xw", [P, 2 * P + 3 * XD])
        xws = sb("xws", [P, 2 * P + 3 * XD])
        wout = sb("wout", [P, C])
        rope_q = sb("rope_q", [P, 2, N])
        rope_k = sb("rope_k", [P, 2, M])
        mask_u8 = sb("mask_u8", [P, M], U8)
        mask_f = sb("mask_f", [P, M])
        mask_row = sb("mask_row", [P, M], BF16)
        any_on = sb("any_on", [P, 1])
        xk_t = sb("xk_t", [P, 2, M])
        xk_parts = sb("xk_parts", [P, 3, M], BF16)
        xv_t = sb("xv_t", [P, M])
        xv = sb("xv", [P, MT, B, XD])
        ones = sb("ones", [P, P])
        kx = [sb(f"kx{i}", [P, B, M], BF16) for i in range(2)]
        qx = [sb(f"qx{i}", [P, B, XH, N], BF16) for i in range(2)]
        xq_t = sb("xq_t", [P, 2, N])
        xq_parts = sb("xq_parts", [P, 2, 3, N], BF16)
        xneg_max = sb("xneg_max", [P, 2, NT, XH])
        xmax_r = sb("xmax_r", [P, NT * XH])
        xmax_parts = sb("xmax_parts", [P, 2, NT, 3, XH], BF16)
        xmax_t = sb("xmax_t", [3 * XH, 2, N], BF16)

        w1 = k_bd[:].rearrange("p b i r n -> p (b i r n)").bitcast(F32)[:, 0:E * F]
        w2 = k_bd[:].rearrange("p b i r n -> p (b i r n)").bitcast(F32)[:, E * F:2 * E * F]
        q_flat = q_st[:].rearrange("p b r n -> p (b r n)").bitcast(F32)
        b1 = q_flat[:, 0:E * FT]
        w1_e = q_flat[:, F:3 * F].rearrange("p (j f) -> p j f", j=2)
        v_flat = v_aug[:].rearrange("p b t i n -> p (b t i n)")
        xs = v_flat[:, 0:BLOCKS * ROW_W].rearrange("p (j c) -> p j c", c=ROW_W)
        xsT = sb("xsT", [P, 2, P])
        hid = probs[:, 0:2, :].rearrange("p s (j f) -> p (s j) f", f=F)
        ys = probs[:, 3, 0:Y_BUFS * C].rearrange("p (j c) -> p j c", c=C)
        wr = sb("wr", [P, E])
        br = sb("br", [P, E])
        route_c = sb("route_c", [P, 3 * 64 + BLOCKS * E])
        tri = sb("tri", [P, P], BF16)
        ones_b = sb("ones_b", [P, P], BF16)
        sc = sb("sc", [P, TT, E])
        cand = sb("cand", [P, TT, E])
        top = sb("top", [P, 2, TT])
        one_hot = sb("one_hot", [P, TT, E], BF16)
        blk = sb("blk", [P, 3, E])
        blk_t = sb("blk_t", [P, BLOCKS, E])
        blk_f = sb("blk_f", [P, BLOCKS])
        block_expert = sb("block_expert", [P, BLOCKS], I32)
        slot_f = sb("slot_f", [P, TT])
        slot = sb("slot", [P, TT], I32)

        ps = ctx.enter_context(nc.psum_tensor("ps", [P, 8, 512], F32))
        s_ring = [ps[:, i, :] for i in range(2)]
        t_ring = [ps[:, 2 + i, :] for i in range(3)]
        o_ps = [ps[:, 5 + i, :] for i in range(2)]
        misc = ps[:, 7, :]

        x_in = [sem(f"x_in{b}") for b in range(B)]
        c_in = sem("c_in")
        c2_in = sem("c2_in")
        c3_in = sem("c3_in")
        mem_in = sem("mem_in")
        dve_step = sem("dve_step")
        act_step = sem("act_step")
        pool_step = sem("pool_step")
        pool_const = sem("pool_const")
        k_zero = sem("k_zero")
        zeroed = sem("zeroed")
        var_ok = sem("var_ok")
        rstd_ok = sem("rstd_ok")
        xn_ok = sem("xn_ok")
        xT_ps = sem("xT_ps")
        xT_ok = sem("xT_ok")
        qk_ps = sem("qk_ps")
        v_ps = sem("v_ps")
        qk_fok = sem("qk_fok")
        v_ok = sem("v_ok")
        parts_ok = sem("parts_ok")
        first_out = sem("first_out")
        parts_out = [sem(f"parts_out{b}") for b in range(B)]
        stacked = [sem(f"stacked{b}") for b in range(B)]
        s_ready = sem("s_ready")
        max_ok = sem("max_ok")
        mparts_ok = sem("mparts_ok")
        mT_ps = sem("mT_ps")
        mT_ok = sem("mT_ok")
        max_out = [sem(f"max_out{b}") for b in range(2 * B)]
        max_in = [sem(f"max_in{b}") for b in range(2 * B)]
        t_ready = sem("t_ready")
        exp_ok = sem("exp_ok")
        pv_ok = sem("pv_ok")
        o_ok = sem("o_ok")
        oT_ps = sem("oT_ps")
        on_ok = sem("on_ok")
        onT_ps = sem("onT_ps")
        onT_ok = sem("onT_ok")
        proj_ps = sem("proj_ps")
        x_ok = sem("x_ok")
        sq_ok = sem("sq_ok")
        mem_rs_ok = sem("mem_rs_ok")
        mem_n_ok = sem("mem_n_ok")
        memT_ps = sem("memT_ps")
        memT_ok = sem("memT_ok")
        kv_ps = sem("kv_ps")
        krope_ok = sem("krope_ok")
        mask_ok = sem("mask_ok")
        xk_ok = sem("xk_ok")
        xvt_ok = sem("xvt_ok")
        xv_ps = sem("xv_ps")
        xv_ok = sem("xv_ok")
        xk_out = sem("xk_out")
        xk_in = sem("xk_in")
        xws_ok = sem("xws_ok")
        xq_ps = sem("xq_ps")
        xrope_ok = sem("xrope_ok")
        xq_ok = sem("xq_ok")
        xq_out = [sem(f"xq_out{b}") for b in range(B)]
        xq_in = [sem(f"xq_in{b}") for b in range(B)]
        xpv_ok = sem("xpv_ok")
        xon_ok = sem("xon_ok")
        ffn_in = sem("ffn_in")
        route_in = sem("route_in")
        xT3_ps = sem("xT3_ps")
        score_ps = sem("score_ps")
        hot_ok = sem("hot_ok")
        rank_ps = sem("rank_ps")
        slot_ok = sem("slot_ok")
        table_ok = sem("table_ok")
        filled = sem("filled")
        scattered = [sem(f"scattered{t}") for t in range(TT)]
        xs_in = [sem(f"xs_in{i}") for i in range(3)]
        xsT_ps = sem("xsT_ps")
        xsT_ok = sem("xsT_ok")
        w1_ok = sem("w1_ok")
        h_ps = sem("h_ps")
        g_ok = sem("g_ok")
        y_ps = sem("y_ps")
        y_ok = sem("y_ok")
        yb_ok = sem("yb_ok")
        out_done = [sem(f"out_done{i}") for i in range(Y_BUFS)]
        ident_ok = sem("ident_ok")

        block = ctx.enter_context(nc.Block())
        W1 = 5 * 16
        W2 = 4 * 16
        W3 = 4 * 16

        @block.sync
        def _(sp):
            sp.dma_start(x[:, 0:NT, :], a["x"][0]).then_inc(x_in[0], 16)
            sp.dma_start(ident[:], a["ident"]).then_inc(c_in, 16)
            sp.dma_start(wqk[:], a["wqk"]).then_inc(c_in, 16)
            sp.dma_start(bqk[:], a["bqk"]).then_inc(c_in, 16)
            for b in range(1, B):
                sp.dma_start(x[:, NT * b:NT * b + NT, :], a["x"][b]).then_inc(x_in[b], 16)
            sp.dma_start(wv[:], a["wv"]).then_inc(c_in, 16)
            sp.dma_start(bv[:], a["bv"]).then_inc(c_in, 16)
            sp.dma_start(mem[:], a["mem"]).then_inc(mem_in, 16)
            for dst, name in ((rms_scale, "rms_scale"), (xw, "xw"), (rope_k, "rope_k"), (mask_u8, "mask")):
                sp.dma_start(dst[:], a[name]).then_inc(c2_in, 16)

            def write_parts(b, parts, written):
                dst = qk_scratch[b, parts].rearrange("s t p n -> p s t n")
                sp.dma_start(dst, qk_parts[:, b, parts]).then_inc(written, 16)

            def stack(b, first):
                for i in range(2):
                    rows = qk_scratch[b].rearrange("s t (d j r) n -> s t j d (r n)", j=2, r=PAIRS)
                    for row, copies, part in Q_COPIES:
                        if (part + copies == 1) != first:
                            continue
                        r = 64 * i + row
                        dst = q_st[r:r + D * copies, b].rearrange("p r n -> p (r n)")
                        sp.dma_start(dst, rows[part:part + copies, 0, i]).then_inc(stacked[b], 16)
                    for row, copies, part in K_COPIES:
                        if (part == 0) != first:
                            continue
                        r = 64 * i + row
                        dst = k_bd[r:r + D * copies, b, i].rearrange("p r n -> p (r n)")
                        src = rows[part:part + 1, 1, i].to_broadcast([copies, D, PAIRS * N])
                        sp.dma_start(dst, src).then_inc(stacked[b], 16)

            def store_parts(b):
                sp.wait_ge(qk_fok, b + 1)
                sp.wait_ge(parts_ok, b + 1)
                write_parts(b, slice(0, 3), parts_out[b])

            def restack(b):
                sp.wait_ge(zeroed, b + 1)
                sp.wait_ge(parts_out[b], 16)
                stack(b, True)
                stack(b, False)

            sp.wait_ge(qk_fok, 1)
            write_parts(0, slice(0, 1), first_out)
            sp.wait_ge(parts_ok, 1)
            write_parts(0, slice(1, 3), parts_out[0])
            sp.wait_ge(zeroed, 1)
            sp.wait_ge(first_out, 16)
            stack(0, True)
            sp.wait_ge(parts_out[0], 16)
            stack(0, False)
            store_parts(1)
            restack(1)
            store_parts(2)
            store_parts(3)
            for dst, name in ((rope_q, "rope_q"), (wout, "wout"), (wproj, "wproj"), (bproj, "bproj")):
                sp.dma_start(dst[:], a[name]).then_inc(c3_in, 16)

            def max_write(b):
                sp.wait_ge(mT_ok, b + 1)
                sp.dma_start(max_scratch[b].rearrange("s i r n -> (s i r) n"), max_t[:, b % 2]).then_inc(max_out[b], 16)

            def max_read(b):
                sp.wait_ge(max_out[b], 16)
                for i in range(2):
                    r = 64 * i + MAX_ROW
                    sp.dma_start(q_st[r:r + 3, b], max_scratch[b, :, i]).then_inc(max_in[b], 16)

            def max_rows(b):
                max_write(b)
                max_read(b)

            def cross_k():
                sp.wait_ge(xk_ok, 1)
                sp.wait_ge(mask_ok, 1)
                sp.dma_start(xk_scratch, xk_parts[:]).then_inc(xk_out, 16)
                sp.dma_start(mask_scratch, mask_row[0:P:XD]).then_inc(xk_out, 16)
                sp.wait_ge(xk_out, 32)
                src = xk_scratch.rearrange("(b d) s m -> s d b m", d=XD)
                for j, row, copies, part in XK_COPIES:
                    for s in range(copies):
                        r = row + XD * s
                        sp.dma_start(kx[j][r:r + XD], src[part]).then_inc(xk_in, 16)
                sp.dma_start(kx[1][XMAX_ROW:XMAX_ROW + 1], mask_scratch.unsqueeze(0)).then_inc(xk_in, 16)

            def xq_write(b):
                sp.wait_ge(xq_ok, b + 1)
                sp.dma_start(xq_scratch[b].rearrange("s p n -> p s n"), xq_parts[:, b % 2]).then_inc(xq_out[b], 16)

            def xq_read(b):
                sp.wait_ge(xq_out[b], 16)
                src = xq_scratch[b].rearrange("s (d h) n -> (s d) (h n)", h=XH)
                for j, row, copies, part in XQ_COPIES:
                    sp.dma_start(qx[j][row:row + XD * copies, b].rearrange("p h n -> p (h n)"),
                                 src[XD * part:XD * (part + copies)]).then_inc(xq_in[b], 16)

            def xmax_write(b):
                sp.wait_ge(mT_ok, B + b + 1)
                sp.dma_start(xmax_scratch[b].rearrange("s h n -> (s h) n"), xmax_t[:, b % 2]).then_inc(max_out[B + b], 16)

            def xmax_read(b):
                sp.wait_ge(max_out[B + b], 16)
                sp.dma_start(qx[0][XMAX_ROW:XMAX_ROW + 3, b], xmax_scratch[b]).then_inc(max_in[B + b], 16)

            max_rows(0)
            restack(2)
            max_rows(1)
            restack(3)
            max_rows(2)
            cross_k()
            sp.dma_start(row_ids[:], a["row_id"]).then_inc(route_in, 16)
            for dst, name in ((wr, "wr"), (br, "br"), (route_c, "route_c"), (tri, "tri"), (ones_b, "ones_b")):
                sp.dma_start(dst[:], a[name]).then_inc(route_in, 16)
            def fill(i):
                j = slice(i * SLOTS // 3, (i + 1) * SLOTS // 3)
                sp.dma_start(sorted_in[j].bitcast(I32), a["empty"][j]).then_inc(filled, 16)

            fill(0)
            fill(1)
            max_write(3)
            xq_write(0)
            max_read(3)
            xq_read(0)
            fill(2)
            xmax_write(0)
            xq_write(1)
            xmax_read(0)
            xq_read(1)
            xmax_write(1)
            xq_write(2)
            xmax_read(1)
            xq_read(2)
            sp.wait_ge(exp_ok, B * H)
            sp.wait_ge(pv_ok, 2 * B)
            sp.dma_start(w1, a["w1"]).then_inc(ffn_in, 16)
            xmax_write(2)
            xq_write(3)
            xmax_read(2)
            xq_read(3)
            sp.dma_start(w2, a["w2"]).then_inc(ffn_in, 16)
            xmax_write(3)
            xmax_read(3)
            sp.dma_start(b1, a["b1"]).then_inc(ffn_in, 16)
            sp.dma_start(b2, a["b2"]).then_inc(ffn_in, 16)
            for t in range(TT):
                sp.wait_ge(scattered[t], 16)
            for i, (j, n) in enumerate(XS_LOADS):
                sp.dma_start(xs[:, j:j + n], sorted_in[P * j:P * (j + n)].rearrange("(j p) c -> p j c", p=P))\
                    .then_inc(xs_in[i], 16)
            for i in range(Y_BUFS):
                sp.wait_ge(out_done[i], 16 * len(range(i, BLOCKS, Y_BUFS)))

        @block.gpsimd
        def _(pool):
            steps = [0]

            def chain(ins):
                steps[0] += 1
                ins.then_inc(pool_step, 1)
                pool.wait_ge(pool_step, steps[0])

            pool.memset(half[:], -0.5).then_inc(pool_const, 1)
            pool.wait_ge(pool_const, 1)

            def power(b, first):
                t = slice(NT * b, NT * b + NT)
                pool.wait_ge(var_ok, first + b + 1)
                if first == B:
                    chain(pool.tensor_tensor(rstd[:, t], var_eps[:, t], half[:, 0:NT], ALU.pow))
                    chain(pool.tensor_tensor(w2nd[:, t], rstd[:, t], rstd[:, t], ALU.mult))
                    chain(pool.tensor_tensor(w2nd[:, t], w2nd[:, t], mv[:, t, 1], ALU.mult))
                    chain(pool.tensor_scalar(w2nd[:, t], w2nd[:, t], RMS_EPS, None, ALU.add))
                    chain(pool.tensor_tensor(w2nd[:, t], w2nd[:, t], half[:, 0:NT], ALU.pow))
                    pool.tensor_tensor(rstd[:, t], rstd[:, t], w2nd[:, t], ALU.mult).then_inc(rstd_ok, 1)
                else:
                    pool.tensor_tensor(rstd[:, t], var_eps[:, t], half[:, 0:NT], ALU.pow).then_inc(rstd_ok, 1)
                pool.wait_ge(rstd_ok, first + b + 1)

            def zero(stack, b):
                chain(pool.memset(stack[:, b].bitcast(F32), 0.0))

            def ones_k(b):
                if b == 0:
                    pool.wait_ge(k_zero, 1)
                chain(pool.memset(k_bd[MAX_ROW:MAX_ROW + 3, b, 0].bitcast(I32), ONE_ONE))
                pool.memset(k_bd[64 + MAX_ROW:64 + MAX_ROW + 3, b, 1].bitcast(I32), ONE_ONE).then_inc(zeroed, 1)
                pool.wait_ge(zeroed, b + 1)

            def zero_v(half):
                b = slice(2 * half, 2 * half + 2)
                chain(pool.memset(v_aug[:, b], 0.0))
                chain(pool.memset(v_aug[:, b, :, 0, 16:17], 1.0))
                pool.memset(v_aug[:, b, :, 1, 17:18], 1.0).then_inc(pool_const, 1)
                pool.wait_ge(pool_const, 2 + half)

            power(0, 0)
            power(1, 0)
            ones_k(0)
            power(2, 0)
            power(3, 0)
            zero_v(0)
            zero_v(1)
            zero(q_st, 1)
            zero(k_bd, 1)
            ones_k(1)
            pool.wait_ge(sq_ok, 1)
            chain(pool.tensor_scalar(mem_rs[:], mem_ss[:], 1.0 / C, RMS_EPS, ALU.mult, ALU.add))
            pool.tensor_tensor(mem_rs[:], mem_rs[:], half[:, 0:B * MT], ALU.pow).then_inc(mem_rs_ok, 1)
            pool.wait_ge(mem_rs_ok, 1)
            for b in range(2, B):
                zero(q_st, b)
                zero(k_bd, b)
                ones_k(b)
            chain(pool.memset(ones[:], 1.0))
            chain(pool.memset(kx[0][XMAX_ROW:XMAX_ROW + 3], 1.0))
            pool.memset(qx[1][XMAX_ROW:XMAX_ROW + 1], 1.0).then_inc(pool_const, 1)
            pool.wait_ge(pool_const, 4)
            pool.wait_ge(krope_ok, 1)
            chain(pool.tensor_tensor(xk_t[:, 0], xk_t[:, 0], xk_t[:, 1], ALU.add))
            chain(pool.tensor_copy(xk_parts[:, 0], xk_t[:, 0]))
            chain(pool.tensor_tensor(xk_t[:, 1], xk_t[:, 0], xk_parts[:, 0], ALU.subtract))
            chain(pool.tensor_copy(xk_parts[:, 1], xk_t[:, 1]))
            pool.tensor_tensor(xk_parts[:, 2], xk_t[:, 1], xk_parts[:, 1], ALU.subtract).then_inc(xk_ok, 1)
            pool.wait_ge(xk_ok, 1)
            for b in range(B):
                power(b, B)
            for b in range(B):
                power(b, 2 * B)
            pool.wait_ge(route_in, 6 * 16)
            chain(pool.tensor_copy(row_id, row_ids[:]))
            pool.wait_ge(filled, 3 * 16)
            pool.wait_ge(slot_ok, 1)
            for t in range(TT):
                pool.indirect_dma_start(
                    out=sorted_in, out_offset=bass.IndirectOffsetOnAxis(ap=slot[:, t:t + 1], axis=0),
                    in_=rows[:, t], in_offset=None).then_inc(scattered[t], 16)
            for j in range(BLOCKS):
                pool.wait_ge(y_ok, j + 1)
                row = xs[:, j, 2 * C:2 * C + 1].bitcast(I32)
                pool.indirect_dma_start(
                    out=a["out"], out_offset=bass.IndirectOffsetOnAxis(ap=row, axis=0),
                    in_=ys[:, j % Y_BUFS], in_offset=None).then_inc(out_done[j % Y_BUFS], 16)

        @block.scalar
        def _(act):
            steps = [0]

            def chain(ins):
                steps[0] += 1
                ins.then_inc(act_step, 1)
                act.wait_ge(act_step, steps[0])

            act.wait_ge(c_in, W1)
            act.activation(bqk_s[:, 1:2], bqk[:, 1:2], ACT.Copy)
            chain(act.mul(bqk_s[:, 0:1], bqk[:, 0:1], SCALE))

            def first_T(b):
                act.wait_ge(xT_ps, b + 1)
                act.activation(xnT[:, NT * b:NT * b + NT, :], ps[:, 6 + b % 2, 0:N], ACT.Copy).then_inc(xT_ok, 1)

            first_T(0)
            for b in range(B):
                if b + 1 < B:
                    first_T(b + 1)
                act.wait_ge(qk_ps, b + 1)
                if b >= 2:
                    act.wait_ge(parts_ok, b - 1)
                for j, s in ((0, SCALE), (1, 1.0)):
                    src = s_ring[b % 2][:, N * j:N * j + N]
                    act.activation(qk_f[:, b % 2, j], src, ACT.Identity, bias=bqk_s[:, j:j + 1], scale=s)
                    last = act.activation(qk_parts[:, b, 0, j], src, ACT.Identity,
                                          bias=bqk_s[:, j:j + 1], scale=s)
                last.then_inc(qk_fok, 1)
                if b >= 1:
                    act.wait_ge(mem_in, 16)
                    for t in ((), range(0, 5), range(5, 10), range(10, B * MT))[b]:
                        last = act.activation(squares[:, t], mem[:, t], ACT.Square, accum_out=mem_ss[:, t:t + 1])
            last.then_inc(sq_ok, 1)
            act.wait_ge(mem_rs_ok, 1)
            for t in range(B * MT):
                last = act.activation(mem[:, t], mem[:, t], ACT.Copy, scale=mem_rs[:, t:t + 1])
            last.then_inc(mem_n_ok, 1)
            act.wait_ge(mem_n_ok, 1)

            def max_copy(b):
                act.wait_ge(mT_ps, b + 1)
                rows, dst = (3 * H, max_t) if b < B else (3 * XH, xmax_t)
                if b % B >= 2:
                    act.wait_ge(max_out[b - 2], 16)
                act.activation(dst[:, b % 2], misc[0:rows, 0:P].bitcast(BF16), ACT.Copy).then_inc(mT_ok, 1)

            def exps(b, p):
                if b >= 1:
                    act.wait_ge(pv_ok, 2 * (b - 1) + p // 4 + 1)
                for i in range(2):
                    g = 2 * (PAIRS * b + p) + i
                    act.wait_ge(t_ready, g + 1)
                    act.activation(probs[:, p, 512 * i:512 * i + 512], t_ring[g % 3], ACT.Exp).then_inc(exp_ok, 1)

            def o_copy(b, g):
                act.wait_ge(pv_ok, 2 * b + g + 1)
                if b >= 1:
                    act.wait_ge(oT_ps, b)
                act.activation(o_sb[:, g], o_ps[g][:, 0:N], ACT.Copy).then_inc(o_ok, 1)

            def normal_T(b):
                act.wait_ge(onT_ps, b + 1)
                if b >= 1:
                    act.wait_ge(proj_ps, b)
                act.activation(o_nT[:], misc[:, 0:N], ACT.Copy).then_inc(onT_ok, 1)

            def cross_T(b):
                act.wait_ge(xT_ps, B + b + 1)
                act.activation(xnT[:, NT * b:NT * b + NT, :], misc[:, 0:N], ACT.Copy).then_inc(xT_ok, 1)

            for i in range(4):
                act.wait_ge(memT_ps, i + 1)
                act.activation(memT[:, 4 * i:4 * i + 4, :], ps[:, 2 + i, :], ACT.Copy).then_inc(memT_ok, 1)
            act.wait_ge(kv_ps, 3)
            act.activation(xv_t[:], ps[:, 4, :], ACT.Copy).then_inc(xvt_ok, 1)
            act.wait_ge(xv_ps, 1)
            act.activation(xv[:], ps[:, 5, :], ACT.Copy).then_inc(xv_ok, 1)
            max_copy(0)
            for b in range(B):
                for p in range(PAIRS):
                    exps(b, p)
                    if b >= 1 and p == 4:
                        o_copy(b - 1, 1)
                    if b >= 1 and p == 0:
                        o_copy(b - 1, 0)
                    if b >= 2 and p == 1:
                        cross_T(b - 2)
                    if p == 4:
                        max_copy(b + 1)
                    if b >= 1 and p == 6:
                        normal_T(b - 1)
            o_copy(B - 1, 0)
            o_copy(B - 1, 1)

            def xexps(b, mt):
                slot = (MT * b + mt) % 8
                if MT * b + mt >= 8:
                    act.wait_ge(xpv_ok, MT * b + mt - 8 + 1)
                else:
                    act.wait_ge(pv_ok, 2 * B)
                for i in range(2):
                    g = B * H + 2 * (MT * b + mt) + i
                    act.wait_ge(t_ready, g + 1)
                    act.activation(probs[:, slot, 512 * i:512 * i + 512], t_ring[g % 3], ACT.Exp).then_inc(exp_ok, 1)

            def router_T(b):
                act.wait_ge(xT3_ps, b + 1)
                act.activation(xnT[:, NT * b:NT * b + NT, :], s_ring[0][:, 0:N], ACT.Copy).then_inc(xT_ok, 1)

            for b in range(B):
                for mt in range(MT):
                    xexps(b, mt)
                    if b < 3 and mt == 2:
                        max_copy(B + b + 1)
                    if (b, mt) == (0, 3):
                        normal_T(B - 1)
                    if b < 2 and mt == 0:
                        cross_T(b + 2)
                    if b == B - 1 and mt != 2:
                        router_T((0, 1, None, 2)[mt])
            router_T(B - 1)
            act.activation(warm[:], ones[:, 0:1], ACT.Gelu)

            def block_T(j):
                act.wait_ge(xsT_ps, j + 1)
                if j >= 2:
                    act.wait_ge(h_ps, j - 1)
                act.activation(xsT[:, j % 2], ps[:, j % 2, 0:P], ACT.Copy).then_inc(xsT_ok, 1)

            block_T(0)
            block_T(1)
            for j in range(BLOCKS):
                act.wait_ge(h_ps, j + 1)
                act.wait_ge(w1_ok, j + 1)
                if j >= 4:
                    act.wait_ge(y_ps, j - 3)
                for f in range(FT):
                    last = act.activation(hid[:, j % 4, P * f:P * f + P],
                                          ps[:, 2 + j % 2, P * f:P * f + P], ACT.Gelu,
                                          bias=b1_e[:, j % 2, f:f + 1])
                last.then_inc(g_ok, 1)
                if j + 2 < BLOCKS:
                    block_T(j + 2)

        @block.vector
        def _(dve):
            steps = [0]

            def chain(ins):
                steps[0] += 1
                ins.then_inc(dve_step, 1)
                dve.wait_ge(dve_step, steps[0])

            def variance(b):
                for t in range(NT * b, NT * b + NT):
                    last = dve.bn_stats(stats[:, t], x[:, t])
                chain(last)
                for t in range(NT * b, NT * b + NT):
                    last = dve.bn_aggr(mv[:, t], stats[:, t])
                chain(last)
                dve.tensor_scalar(var_eps[:, NT * b:NT * b + NT], mv[:, NT * b:NT * b + NT, 1], LN_EPS, None,
                                  ALU.add).then_inc(var_ok, 1)

            def normal(b, first):
                dve.wait_ge(rstd_ok, first + b + 1)
                if first:
                    dve.wait_ge(xT_ps, first - B + b + 1)
                for t in range(NT * b, NT * b + NT):
                    last = dve.tensor_scalar(xn[:, t], x[:, t], mv[:, t, 0:1], rstd[:, t:t + 1],
                                             ALU.subtract, ALU.mult)
                last.then_inc(xn_ok, 1)

            def split(b):
                dve.wait_ge(qk_fok, b + 1)
                if b >= 1:
                    dve.wait_ge(parts_ok, b)
                whole = qk_f[:, b % 2].rearrange("p a n -> p (a n)")
                part = [qk_parts[:, b, s].rearrange("p a n -> p (a n)") for s in range(3)]
                chain(dve.tensor_tensor(qk_r[:], whole, part[0], ALU.subtract))
                chain(dve.tensor_copy(part[1], qk_r[:]))
                dve.tensor_tensor(part[2], qk_r[:], part[1], ALU.subtract).then_inc(parts_ok, 1)

            def values(b):
                dve.wait_ge(v_ps, b + 1)
                src = ps[:, 2 + b, 0:NT * P].rearrange("p (t i d) -> p t i d", i=2, d=D)
                bias = bv[:].rearrange("p a (t i d) -> p (a t) i d", i=2, d=D)
                for i in range(2):
                    last = dve.tensor_tensor(v_aug[:, b, :, i, D * i:D * i + D], src[:, :, i],
                                             bias[:, :, i], ALU.add)
                last.then_inc(v_ok, 1)

            dve.memset(q_st[:, 0].bitcast(F32), 0.0)
            dve.memset(k_bd[:, 0].bitcast(F32), 0.0).then_inc(k_zero, 1)
            for b in range(B):
                dve.wait_ge(x_in[b], 16)
                variance(b)
                if b >= 1:
                    normal(b - 1, 0)
            normal(B - 1, 0)
            for b in range(B):
                split(b)
                if b == 1:
                    dve.wait_ge(c2_in, W2)
                    dve.scalar_tensor_tensor(xws[:], xw[:], rms_scale[:], xw[:], ALU.mult, ALU.add).then_inc(xws_ok, 1)
                if b >= 1:
                    dve.wait_ge(pool_const, 2 + (b - 1) // 2)
                    values(b - 1)
            values(B - 1)
            dve.wait_ge(c_in, W1)
            dve.tensor_copy(ident_b[:], ident[:]).then_inc(ident_ok, 1)
            def maxima(g):
                b, c = divmod(g, CHUNKS)
                nt, pair = divmod(c, PAIRS)
                dve.wait_ge(s_ready, g + 1)
                if c == 0 and b >= 2:
                    dve.wait_ge(mparts_ok, b - 1)
                dve.tensor_reduce(neg_max[:, b % 2, nt, :, pair], s_ring[g % 2].rearrange("p (i m) -> p i m", i=2),
                                  AX.X, ALU.max, negate=True).then_inc(max_ok, 1)

            def split_max(b, whole, rest, parts, seen):
                dve.wait_ge(max_ok, seen)
                if b % B >= 1:
                    dve.wait_ge(mparts_ok, b)
                if b % B >= 2:
                    dve.wait_ge(mT_ps, b - 1)
                view = rest.rearrange("p (a h) -> p a h", a=NT)
                chain(dve.tensor_copy(parts[:, :, 0], whole))
                chain(dve.tensor_tensor(view, whole, parts[:, :, 0], ALU.subtract))
                chain(dve.tensor_copy(parts[:, :, 1], view))
                dve.tensor_tensor(parts[:, :, 2], view, parts[:, :, 1], ALU.subtract).then_inc(mparts_ok, 1)

            def max_split(b):
                split_max(b, neg_max[:, b % 2].rearrange("p a i r -> p a (i r)"), max_r[:], max_parts[:, b % 2],
                          CHUNKS * (b + 1))

            def context():
                chain(dve.tensor_copy(mask_f[:], mask_u8[:]))
                chain(dve.tensor_reduce(any_on[:], mask_f[:], AX.X, ALU.max))
                dve.wait_ge(kv_ps, 3)
                dve.scalar_tensor_tensor(xk_t[:, 0], ps[:, 2, :], any_on[:], rope_k[:, 0], ALU.mult, ALU.mult)
                dve.scalar_tensor_tensor(xk_t[:, 1], ps[:, 3, :], any_on[:], rope_k[:, 1], ALU.mult,
                                         ALU.mult).then_inc(krope_ok, 1)

            def normalise(b):
                dve.wait_ge(oT_ps, b + 1)
                if b >= 1:
                    dve.wait_ge(onT_ps, b)
                heads = misc.rearrange("p (q c) -> p q c", c=32)
                sums = rec[:, 0:NT * H].rearrange("p (q i) -> p q i", i=2)
                chain(dve.reciprocal(sums, heads[:, :, 2 * D:2 * D + 2]))
                dve.tensor_tensor(o_n[:].rearrange("p (q i d) -> p q i d", i=2, d=D),
                                  heads[:, :, 0:2 * D].rearrange("p q (i d) -> p q i d", d=D),
                                  sums.unsqueeze(3).to_broadcast([P, NT * PAIRS, 2, D]), ALU.mult).then_inc(on_ok, 1)

            def residual(b, first):
                dve.wait_ge(proj_ps, first + b + 1)
                t = x[:, NT * b:NT * b + NT, :]
                dve.tensor_tensor(t, t, misc[:, 0:N].rearrange("p (a n) -> p a n", a=NT), ALU.add).then_inc(x_ok, 1)
                dve.wait_ge(x_ok, first + b + 1)

            def cross_q(b):
                dve.wait_ge(xq_ps, b + 1)
                if b == 0:
                    dve.wait_ge(c3_in, W3)
                if b >= 1:
                    dve.wait_ge(xq_ok, b)
                if b >= 2:
                    dve.wait_ge(xq_out[b - 2], 16)
                dve.tensor_tensor(xq_t[:, 0], misc[:, 0:N], rope_q[:, 0], ALU.mult)
                dve.tensor_tensor(xq_t[:, 1], misc[:, N:2 * N], rope_q[:, 1], ALU.mult).then_inc(xrope_ok, 1)

            def cross_q_parts(b):
                dve.wait_ge(xrope_ok, b + 1)
                part = [xq_parts[:, b % 2, s] for s in range(3)]
                chain(dve.tensor_tensor(xq_t[:, 0], xq_t[:, 0], xq_t[:, 1], ALU.add))
                chain(dve.tensor_copy(part[0], xq_t[:, 0]))
                chain(dve.tensor_tensor(xq_t[:, 1], xq_t[:, 0], part[0], ALU.subtract))
                chain(dve.tensor_copy(part[1], xq_t[:, 1]))
                dve.tensor_tensor(part[2], xq_t[:, 1], part[1], ALU.subtract).then_inc(xq_ok, 1)

            def xmaxima(g):
                b, c = divmod(g, XCHUNKS)
                nt, h = divmod(c, XH)
                g += B * CHUNKS
                dve.wait_ge(s_ready, g + 1)
                if c == 0 and b >= 2:
                    dve.wait_ge(mparts_ok, B + b - 1)
                dve.tensor_reduce(xneg_max[:, b % 2, nt, h:h + 1], s_ring[g % 2], AX.X, ALU.max,
                                  negate=True).then_inc(max_ok, 1)
                if c == XCHUNKS - 1:
                    split_max(B + b, xneg_max[:, b % 2], xmax_r[:], xmax_parts[:, b % 2],
                              B * CHUNKS + XCHUNKS * (b + 1))

            def next_maxima(g):
                maxima(g)
                if g % CHUNKS == CHUNKS - 1:
                    max_split(g // CHUNKS)

            for g in range(CHUNKS):
                next_maxima(g)
            context()
            for g in range(CHUNKS, CHUNKS + LEAD):
                next_maxima(g)
            for b in range(B):
                for p in range(PAIRS):
                    for g in range(CHUNKS + LEAD + 2 * (PAIRS * b + p), CHUNKS + LEAD + 2 * (PAIRS * b + p) + 2):
                        if g < B * CHUNKS:
                            next_maxima(g)
                    if b == B - 1:
                        for g in XFIRST[p]:
                            xmaxima(g)
                    if b == 0 and p == 1:
                        dve.tensor_scalar(mask_row[:], mask_f[:], any_on[:], -MASK_FILL, ALU.subtract,
                                          ALU.mult).then_inc(mask_ok, 1)
                    if b >= 2 and p == 0:
                        normal(b - 2, B)
                    if b >= 2 and p == 2:
                        cross_q(b - 2)
                    if b >= 2 and p == 4:
                        cross_q_parts(b - 2)
                    if b >= 1 and p == 5:
                        normalise(b - 1)
                    if b >= 1 and p == 7:
                        residual(b - 1, 0)
                        variance(b - 1)
            for p in range(4):
                for g in XFIRST[PAIRS + p]:
                    xmaxima(g)
            normal(B - 2, B)

            def xnormalise(b):
                dve.wait_ge(xpv_ok, MT * (b + 1))
                dve.wait_ge(proj_ps, B + b)
                chain(dve.reciprocal(rec[:], o_ps[b % 2][:, N:2 * N]))
                dve.tensor_tensor(o_n[:], o_ps[b % 2][:, 0:N], rec[:], ALU.mult).then_inc(xon_ok, 1)

            for b in range(B):
                for mt in range(MT):
                    for g in XAHEAD.get((b, mt), ()):
                        xmaxima(g)
                    if (b, mt) == (0, 1):
                        cross_q(2)
                        cross_q_parts(2)
                    if (b, mt) == (0, 2):
                        normalise(B - 1)
                    if (b, mt) == (0, 3):
                        residual(B - 1, 0)
                        variance(B - 1)
                    if (b, mt) == (1, 0):
                        normal(B - 1, B)
                    if b >= 1 and mt == (0, 2, 1, 0)[b]:
                        xnormalise(b - 1)
                    if (b, mt) == (1, 1):
                        cross_q(3)
                        cross_q_parts(3)
                    if b >= 1 and mt == (0, 3, 2, 1)[b]:
                        residual(b - 1, B)
                        variance(b - 1)
                    if (b, mt) in ((2, 1), (2, 3), (3, 2)):
                        normal(((2, 1), (2, 3), (3, 2)).index((b, mt)), 2 * B)
            xnormalise(B - 1)
            residual(B - 1, B)
            variance(B - 1)
            normal(B - 1, 2 * B)

            table = [route_c[:, 64 * i:64 * i + 64].rearrange("p (a e) -> p a e", e=E) for i in range(3)]
            rank_down, steps128, before = table
            block_no = route_c[:, 192:192 + BLOCKS * E].rearrange("p (j e) -> p j e", e=E)
            dve.wait_ge(route_in, 6 * 16)
            dve.wait_ge(score_ps, 1)
            chain(dve.tensor_tensor(sc[:], s_ring[1][:, 0:TT * E].rearrange("p (t e) -> p t e", e=E),
                                    br[:].unsqueeze(1).to_broadcast([P, TT, E]), ALU.add))
            chain(dve.tensor_reduce(top[:, 0], sc[:], AX.X, ALU.max))
            chain(dve.tensor_tensor(cand[:], sc[:], top[:, 0].unsqueeze(2).to_broadcast([P, TT, E]), ALU.is_ge))
            chain(dve.tensor_tensor(cand[:], cand[:], rank_down, ALU.mult))
            chain(dve.tensor_reduce(top[:, 1], cand[:], AX.X, ALU.max))
            dve.tensor_tensor(one_hot[:], cand[:], top[:, 1].unsqueeze(2).to_broadcast([P, TT, E]),
                              ALU.is_equal).then_inc(hot_ok, 1)
            dve.wait_ge(rank_ps, 1)
            rank = ps[:, 0, 0:TT * E].rearrange("p (t e) -> p t e", e=E)
            chain(dve.tensor_tensor(sc[:], ps[:, 0, TT * E:TT * E + E].unsqueeze(2).to_broadcast([P, E, TT]),
                                    steps128, ALU.is_gt))
            chain(dve.tensor_reduce(blk[:, 0], sc[:], AX.X, ALU.add))
            chain(dve.tensor_tensor(sc[:], blk[:, 0].unsqueeze(1).to_broadcast([P, E, E]), before, ALU.mult))
            chain(dve.tensor_reduce(blk[:, 1], sc[:], AX.X, ALU.add))
            chain(dve.scalar_tensor_tensor(cand[:], blk[:, 1].unsqueeze(1).to_broadcast([P, TT, E]), float(P),
                                           rank, ALU.mult, ALU.add))
            chain(dve.tensor_tensor(cand[:], cand[:], one_hot[:], ALU.mult))
            chain(dve.tensor_reduce(slot_f[:], cand[:], AX.X, ALU.add))
            dve.tensor_copy(slot[:], slot_f[:]).then_inc(slot_ok, 1)
            chain(dve.tensor_tensor(blk[:, 2], blk[:, 0], blk[:, 1], ALU.add))
            chain(dve.tensor_tensor(blk_t[:], blk[:, 2].unsqueeze(1).to_broadcast([P, BLOCKS, E]), block_no,
                                    ALU.is_le))
            chain(dve.tensor_reduce(blk_f[:], blk_t[:], AX.X, ALU.add))
            dve.tensor_scalar(block_expert[:], blk_f[:], float(E - 1), None, ALU.min).then_inc(table_ok, 1)
            dve.wait_ge(table_ok, 1)
            dve.wait_ge(ffn_in, 4 * 16)

            def pick(j):
                e = dve.value_load(block_expert[0:1, j:j + 1], min_val=0, max_val=E - 1)
                if j >= 2:
                    dve.wait_ge(h_ps, j - 1)
                    dve.wait_ge(g_ok, j - 1)
                dve.tensor_copy(b1_e[:, j % 2], b1[:, bass.ds(e * FT, FT)])
                dve.tensor_copy(w1_e[:, j % 2], w1[:, bass.ds(e * F, F)]).then_inc(w1_ok, 1)

            def block_out(j):
                e = dve.value_load(block_expert[0:1, j:j + 1], min_val=0, max_val=E - 1)
                dve.wait_ge(y_ps, j + 1)
                if j >= Y_BUFS:
                    dve.wait_ge(out_done[j % Y_BUFS], 16 * (j // Y_BUFS))
                y = ys[:, j % Y_BUFS]
                dve.tensor_tensor(y, ps[:, 6 + j % 2, 0:C], b2[:, bass.ds(e * C, C)], ALU.add).then_inc(yb_ok, 1)
                dve.wait_ge(yb_ok, j + 1)
                dve.tensor_tensor(y, y, xs[:, j, C:2 * C], ALU.add).then_inc(y_ok, 1)

            pick(0)
            pick(1)
            for j in range(BLOCKS):
                if j >= 1 and j + 1 < BLOCKS:
                    pick(j + 1)
                if j >= 2:
                    block_out(j - 2)
            block_out(BLOCKS - 2)
            block_out(BLOCKS - 1)

        @block.tensor
        def _(pe):
            mm = nc.tensor.matmul

            def transposes(b, first, half):
                pe.wait_ge(xn_ok, first + b + 1)
                for t in range(NT):
                    last = nc.tensor.transpose(half[:, P * t:P * t + P], xn[:, NT * b + t], ident[:])
                last.then_inc(xT_ps, 1)

            def project(b):
                pe.wait_ge(xT_ok, b + 1)
                if b >= 2:
                    pe.wait_ge(qk_fok, b - 1)
                rhs = xnT[:, NT * b:NT * b + NT, :].rearrange("p t n -> p (t n)")
                for j in range(2):
                    last = mm(s_ring[b % 2][:, N * j:N * j + N], wqk[:, j], rhs, start=True, stop=True)
                last.then_inc(qk_ps, 1)
                for t in range(NT):
                    last = mm(ps[:, 2 + b, P * t:P * t + P], xnT[:, NT * b + t], wv[:], start=True, stop=True)
                last.then_inc(v_ps, 1)

            pe.wait_ge(c_in, W1)
            transposes(0, 0, ps[:, 6, :])
            for b in range(B):
                if b + 1 < B:
                    if b >= 1:
                        pe.wait_ge(xT_ok, b)
                    transposes(b + 1, 0, ps[:, 6 + (b + 1) % 2, :])
                project(b)

            def scores(g):
                b, c = divmod(g, CHUNKS)
                nt, pair = divmod(c, PAIRS)
                if c == 0:
                    pe.wait_ge(stacked[b], 12 * 16)
                if g == 0:
                    pe.wait_ge(qk_fok, B)
                if g >= 2:
                    pe.wait_ge(max_ok, g - 1)
                mm(s_ring[g % 2], q_st[:, b, pair, P * nt:P * nt + P],
                   k_bd[:, b, :, pair], start=True, stop=True).then_inc(s_ready, 1)

            def max_transposes(b):
                pe.wait_ge(mparts_ok, b + 1)
                if b == 0:
                    pe.wait_ge(xT_ok, B)
                    pe.wait_ge(ident_ok, 1)
                elif b <= 2:
                    pe.wait_ge(mT_ok, b)
                elif b <= B:
                    pe.wait_ge(xrope_ok, b - 2)
                elif b < B + 3:
                    pe.wait_ge(xrope_ok, b - B + 2)
                else:
                    pe.wait_ge(x_ok, B + 1)
                rows, src = (3 * H, max_parts) if b < B else (3 * XH, xmax_parts)
                for nt in range(NT):
                    last = nc.tensor.transpose(misc[0:rows, 64 * nt:64 * nt + 64].bitcast(BF16),
                                               src[:, b % 2, nt].rearrange("p s h -> p (s h)"), ident_b[:])
                last.then_inc(mT_ps, 1)

            def context_T(i):
                pe.wait_ge(mem_n_ok, 1)
                pe.wait_ge(v_ok, B)
                for t in range(4):
                    last = nc.tensor.transpose(ps[:, 2 + i, P * t:P * t + P], mem[:, 4 * i + t], ident[:])
                last.then_inc(memT_ps, 1)

            def context_kv(j):
                pe.wait_ge(memT_ok, 4)
                pe.wait_ge(xws_ok, 1)
                w = xws[:, 2 * P + XD * j:2 * P + XD * j + XD]
                for b in range(B):
                    last = mm(ps[XD * b:XD * b + XD, 2 + j, :], w,
                              memT[:, MT * b:MT * b + MT, :].rearrange("p t n -> p (t n)"),
                              start=True, stop=True)
                last.then_inc(kv_ps, 1)

            def context_vT():
                pe.wait_ge(xvt_ok, 1)
                for t in range(MT):
                    last = nc.tensor.transpose(ps[:, 5, P * t:P * t + P], xv_t[:, P * t:P * t + P], ident[:])
                last.then_inc(xv_ps, 1)

            def weights(b, p):
                if p == 0:
                    pe.wait_ge(max_in[b], 2 * 16)
                if b == 0 and p == 0:
                    pe.wait_ge(krope_ok, 1)
                    pe.wait_ge(xv_ok, 1)
                for i in range(2):
                    g = 2 * (PAIRS * b + p) + i
                    if g >= 3:
                        pe.wait_ge(exp_ok, g - 2)
                    for mt in range(NT):
                        last = mm(t_ring[g % 3][:, N * mt:N * mt + N], k_bd[:, b, i, p, P * mt:P * mt + P],
                                  q_st[:, b, p], start=True, stop=True)
                    last.then_inc(t_ready, 1)

            def attend(b, g, r):
                i, mt = divmod(r, NT)
                if r == 0:
                    pe.wait_ge(exp_ok, 2 * (PAIRS * b + 4 * g + 4))
                    if b >= 1:
                        pe.wait_ge(o_ok, 2 * (b - 1) + g + 1)
                for q in range(4):
                    p = 4 * g + q
                    last = mm(o_ps[g][32 * q:32 * q + 32, 0:N], v_aug[:, b, PAIRS * mt + p, i],
                              probs[:, p, 512 * i + N * mt:512 * i + N * mt + N], start=(r == 0), stop=(r == 3))
                if r == 3:
                    last.then_inc(pv_ok, 1)

            def tokens_T(b):
                pe.wait_ge(o_ok, 2 * b + 2)
                pe.wait_ge(mT_ok, b + 3)
                for nt in range(NT):
                    for g in range(2):
                        last = nc.tensor.transpose(misc[:, P * (2 * nt + g):P * (2 * nt + g) + P],
                                                   o_sb[:, g, P * nt:P * nt + P], ident[:])
                last.then_inc(oT_ps, 1)

            def normal_T(b):
                pe.wait_ge(on_ok, b + 1)
                for nt in range(NT):
                    last = nc.tensor.transpose(misc[:, P * nt:P * nt + P], o_n[:, P * nt:P * nt + P], ident[:])
                last.then_inc(onT_ps, 1)

            def output(b):
                pe.wait_ge(onT_ok, b + 1)
                if b == 0:
                    pe.wait_ge(c3_in, W3)
                    pe.wait_ge(pool_const, 4)
                for nt in range(NT):
                    mm(misc[:, P * nt:P * nt + P], o_nT[:, P * nt:P * nt + P], wproj[:], start=True, stop=False)
                    last = mm(misc[:, P * nt:P * nt + P], ones[0:1, :], bproj[:], start=False, stop=True)
                last.then_inc(proj_ps, 1)

            def cross_T(b):
                transposes(b, B, misc)

            def cross_project(b):
                pe.wait_ge(xT_ok, B + b + 1)
                rhs = xnT[:, NT * b:NT * b + NT, :].rearrange("p t n -> p (t n)")
                for j in range(2):
                    last = mm(misc[:, N * j:N * j + N], xws[:, P * j:P * j + P], rhs, start=True, stop=True)
                last.then_inc(xq_ps, 1)

            def xscores(g):
                b, c = divmod(g, XCHUNKS)
                nt, h = divmod(c, XH)
                g += B * CHUNKS
                if c == 0:
                    pe.wait_ge(xq_in[b], 3 * 16)
                if b == 0 and c == 0:
                    pe.wait_ge(xk_in, 7 * 16)
                    pe.wait_ge(pool_const, 4)
                pe.wait_ge(max_ok, g - 1)
                mm(s_ring[g % 2], qx[0][0:96, b, h, P * nt:P * nt + P], kx[0][0:96, b], start=True, stop=False)
                mm(s_ring[g % 2], qx[1][0:97, b, h, P * nt:P * nt + P], kx[1][0:97, b],
                   start=False, stop=True).then_inc(s_ready, 1)

            for g in range(CHUNKS + LEAD):
                if 9 <= g < 13:
                    context_T(g - 9)
                if 14 <= g < 17:
                    context_kv(g - 14)
                if g == CHUNKS + 1:
                    context_vT()
                if g == CHUNKS + 2:
                    max_transposes(0)
                scores(g)
            for b in range(B):
                for p in range(PAIRS):
                    weights(b, p)
                    if p < 4 and b >= 1:
                        attend(b - 1, 1, p)
                    if p >= 4:
                        attend(b, 0, p - 4)
                    for g in range(CHUNKS + LEAD + 2 * (PAIRS * b + p), CHUNKS + LEAD + 2 * (PAIRS * b + p) + 2):
                        if g < B * CHUNKS:
                            scores(g)
                    if b == B - 1:
                        for g in XFIRST[p]:
                            xscores(g)
                    if p == 1 and b >= 2:
                        cross_T(b - 2)
                    if p == 2 and b >= 2:
                        cross_project(b - 2)
                    if p == 4:
                        max_transposes(b + 1)
                    if p == 5 and b >= 1:
                        tokens_T(b - 1)
                    if p == 6 and b >= 1:
                        normal_T(b - 1)
                    if p == 7 and b >= 1:
                        output(b - 1)
            for p in range(4):
                attend(B - 1, 1, p)
                for g in XFIRST[PAIRS + p]:
                    xscores(g)

            def xweights(b, mt):
                if mt == 0:
                    pe.wait_ge(max_in[B + b], 16)
                for pair in range(2):
                    g = B * H + 2 * (MT * b + mt) + pair
                    pe.wait_ge(exp_ok, g - 2)
                    for j, rows in ((0, 99), (1, 97)):
                        last = mm(t_ring[g % 3], kx[j][0:rows, b, P * mt:P * mt + P],
                                  qx[j][0:rows, b, 2 * pair:2 * pair + 2].rearrange("p h n -> p (h n)"),
                                  start=(j == 0), stop=(j == 1))
                    last.then_inc(t_ready, 1)

            def xattend(b, mt):
                g = MT * b + mt
                pe.wait_ge(exp_ok, B * H + 2 * (g + 1))
                if mt == 0 and b < 2:
                    pe.wait_ge(o_ok, 2 * B - 1 + b)
                elif mt == 0:
                    pe.wait_ge(xon_ok, b - 1)
                for what in range(2):
                    for h in range(XH):
                        last = mm(o_ps[b % 2][32 * h:32 * h + 32, N * what:N * what + N],
                                  ones[:, 0:XD] if what else xv[:, mt, b], probs[:, g % 8, N * h:N * h + N],
                                  start=(mt == 0 and what == 0), stop=(mt == MT - 1), skip_group_check=True)
                last.then_inc(xpv_ok, 1)

            def xoutput(b):
                pe.wait_ge(xon_ok, b + 1)
                pe.wait_ge(mT_ok, min(B + b + 3, 2 * B))
                if b >= 2:
                    pe.wait_ge(x_ok, B + b)
                for nt in range(NT):
                    last = mm(misc[:, P * nt:P * nt + P], o_n[:, P * nt:P * nt + P], wout[:],
                              start=True, stop=True)
                last.then_inc(proj_ps, 1)

            def router_T(b):
                pe.wait_ge(xn_ok, 2 * B + b + 1)
                if b == 0:
                    pe.wait_ge(max_ok, B * (CHUNKS + XCHUNKS))
                else:
                    pe.wait_ge(xT_ok, 2 * B + b)
                for t in range(NT):
                    last = nc.tensor.transpose(s_ring[0][:, P * t:P * t + P], xn[:, NT * b + t], ident[:])
                last.then_inc(xT3_ps, 1)

            def router(b, end=False):
                pe.wait_ge(route_in, 6 * 16)
                pe.wait_ge(xT_ok, 2 * B + b + 1)
                for t in range(NT * b, NT * b + NT):
                    last = mm(s_ring[1][:, E * t:E * t + E], xnT[:, t], wr[:], start=True, stop=True)
                if end:
                    last.then_inc(score_ps, 1)

            for b in range(B):
                for mt in range(MT):
                    xweights(b, mt)
                    if b < 3 and mt == 2:
                        max_transposes(B + b + 1)
                    if mt or b:
                        g = MT * b + mt - 1
                        xattend(g // MT, g % MT)
                    if (b, mt) == (0, 3):
                        normal_T(B - 1)
                    for g in XAHEAD.get((b, mt), ()):
                        xscores(g)
                    if (b, mt) in ((0, 0), (1, 0)):
                        cross_T(b + 2)
                    if (b, mt) in ((0, 1), (1, 1)):
                        cross_project(b + 2)
                    if (b, mt) == (0, 2):
                        tokens_T(B - 1)
                    if (b, mt) == (0, 3):
                        output(B - 1)
                    if b == B - 1 and mt in (1, 3):
                        router(mt // 2)
                    if b == B - 1 and mt != 2:
                        router_T((0, 1, None, 2)[mt])
                    if b >= 1 and mt == (0, 3, 2, 1)[b]:
                        xoutput(b - 1)
            xattend(B - 1, MT - 1)
            router(B - 2)
            xoutput(B - 1)
            router_T(B - 1)
            router(B - 1, True)
            pe.wait_ge(hot_ok, 1)
            hot = one_hot[:].rearrange("p t e -> p (t e)")
            mm(ps[:, 0, 0:TT * E], tri[:], hot, start=True, stop=False, skip_group_check=True)
            for t in range(TT):
                last = mm(ps[:, 0, E * (t + 1):E * (TT + 1)].rearrange("p (a e) -> p a e", e=E), ones_b[:],
                          one_hot[:, t:t + 1].to_broadcast([P, TT - t, E]), start=False, stop=(t == TT - 1),
                          skip_group_check=True)
            last.then_inc(rank_ps, 1)

            def block_T(j):
                for i, (first, _) in enumerate(XS_LOADS):
                    if j == first:
                        pe.wait_ge(xs_in[i], 16)
                if j >= 2:
                    pe.wait_ge(xsT_ok, j - 1)
                nc.tensor.transpose(ps[:, j % 2, 0:P], xs[:, j, 0:C], ident[:]).then_inc(xsT_ps, 1)

            def block_h(j):
                pe.wait_ge(xsT_ok, j + 1)
                pe.wait_ge(w1_ok, j + 1)
                if j >= 2:
                    pe.wait_ge(g_ok, j - 1)
                for f in range(FT):
                    last = mm(ps[:, 2 + j % 2, P * f:P * f + P], w1_e[:, j % 2, P * f:P * f + P], xsT[:, j % 2],
                              start=True, stop=True)
                last.then_inc(h_ps, 1)

            def block_y(j):
                e = pe.value_load(block_expert[0:1, j:j + 1], min_val=0, max_val=E - 1)
                pe.wait_ge(g_ok, j + 1)
                if j >= 2:
                    pe.wait_ge(yb_ok, j - 1)
                for f in range(FT):
                    last = mm(ps[:, 6 + j % 2, 0:C], hid[:, j % 4, P * f:P * f + P],
                              w2[:, bass.ds(e * F + f * C, C)], start=(f == 0), stop=(f == FT - 1))
                last.then_inc(y_ps, 1)

            pe.wait_ge(table_ok, 1)
            pe.wait_ge(ffn_in, 4 * 16)
            block_T(0)
            block_T(1)
            block_h(0)
            for j in range(BLOCKS):
                if j + 1 < BLOCKS:
                    block_h(j + 1)
                if j + 2 < BLOCKS:
                    block_T(j + 2)
                if j >= 1:
                    block_y(j - 1)
            block_y(BLOCKS - 1)


def layout(inputs):
    i = {k: np.asarray(v) for k, v in inputs.items()}
    order = np.arange(C).reshape(PAIRS, 2, D).transpose(2, 1, 0).reshape(-1)
    wqkv, bqkv = i["L0_attn_w_qkv"], i["L0_attn_b_qkv"]
    wqk = np.stack([wqkv[0:C].T[:, order], wqkv[C:2 * C].T[:, order]], 1)
    bqk = np.stack([bqkv[0:C][order], bqkv[C:2 * C][order]], 1)
    swap = (np.arange(XD) + XD // 2) % XD
    wq = i["L0_xattn_q_w"].transpose(1, 2, 0)
    wk, wv = i["L0_xattn_kv_w"][0, 0], i["L0_xattn_kv_w"][1, 0]
    xw = np.concatenate([wq.reshape(C, -1), wq[:, swap].reshape(C, -1), wk, wk[:, swap], wv], 1)
    freq = (np.float32(10000.0) ** (np.float32(2.0 / XD) * np.arange(XD // 2, dtype=np.float32))).astype(np.float32)

    def rope(positions, scale):
        angle = positions.astype(np.float32)[None, :] / freq[:, None]
        cos, sin = np.cos(angle), np.sin(angle)
        t = np.stack([np.concatenate([cos, cos]), np.concatenate([-sin, sin])], 1) * np.float32(scale)
        return t.astype(np.float32)

    a = {
        "x": i["x"].reshape(B, NT, P, C).transpose(0, 2, 1, 3),
        "ident": np.eye(P, dtype=np.float32),
        "wqk": wqk, "bqk": bqk, "wv": wqkv[2 * C:].T,
        "bv": np.broadcast_to(bqkv[2 * C:], (P, NT, C)),
        "wproj": i["L0_attn_w_proj"].T, "bproj": i["L0_attn_b_proj"].reshape(1, C),
        "mem": i["ctx_1024"].reshape(B * MT, P, C).transpose(1, 0, 2),
        "mask": np.repeat(i["mask_BxS2_bk0"], XD, axis=0),
        "rms_scale": i["L0_xattn_rms_scale"].reshape(C, 1),
        "xw": xw, "wout": i["L0_xattn_out_w"].reshape(XH * XD, C),
        "rope_q": np.repeat(rope(np.arange(M, M + N), XD ** -0.5), XH, axis=0),
        "rope_k": np.tile(rope(np.arange(M), 1.0), (B, 1, 1)),
    }
    empty = np.zeros((SLOTS, ROW_W), np.int32)
    empty[:, 2 * C] = B * N + np.arange(SLOTS)
    w1, w2 = i["L0_ffn_w1"], i["L0_ffn_w2"]
    t, e = np.arange(TT), np.arange(E)
    route = np.concatenate([
        np.tile(E - e, TT), np.tile(P * t, E), (e[None, :] < e[:, None]).reshape(-1), np.repeat(np.arange(BLOCKS), E)])
    a.update({
        "row_id": np.arange(TT * P, dtype=np.int32).reshape(TT, P).T,
        "empty": empty,
        "w1": w1.transpose(1, 0, 2).reshape(P, E * F),
        "w2": w2.reshape(E, FT, P, C).transpose(2, 0, 1, 3).reshape(P, E * F),
        "b1": i["L0_ffn_b1"].reshape(E, FT, P).transpose(2, 0, 1).reshape(P, E * FT),
        "b2": np.broadcast_to(i["L0_ffn_b2"].reshape(-1), (P, E * C)),
        "wr": i["L0_ffn_wr"],
        "br": np.broadcast_to(i["L0_ffn_br"], (P, E)),
        "route_c": np.broadcast_to(route.astype(np.float32), (P, route.size)),
        "tri": np.triu(np.ones((P, P)), 1).astype(mybir.dt.np(BF16)),
        "ones_b": np.ones((P, P), mybir.dt.np(BF16)),
    })
    return {k: np.ascontiguousarray(v) for k, v in a.items()}


def kernel(**inputs):
    import concourse.bacc as bacc
    from concourse.bass_utils import run_bass_kernel_spmd

    nc = bacc.Bacc("TRN2", target_bir_lowering=False, num_devices=1)
    arrays = layout(inputs)
    a = {k: nc.dram_tensor("in_" + k, v.shape, mybir.dt.from_np(v.dtype), kind="ExternalInput").ap()
         for k, v in arrays.items()}
    a["out"] = nc.dram_tensor("out", (B * N + SLOTS, C), F32, kind="ExternalOutput").ap()
    build(nc, a)
    r = run_bass_kernel_spmd(nc, [{"in_" + k: v for k, v in arrays.items()}], core_ids=[0])
    y = r.results[0]["out"][0:B * N].reshape(B, N, C)
    return np.ascontiguousarray(y)
```
